# Optimizing a Trainium2 kernel written in Bass

```python
import numpy as np
import jax
import jax.numpy as jnp

def _softmax(x, axis=-1):
    return jax.nn.softmax(x, axis=axis)

def _gelu(x):
    return jax.nn.gelu(x, approximate=True)

def _silu(x):
    return jax.nn.silu(x)

def _sigmoid(x):
    return jax.nn.sigmoid(x)

def _layernorm(x, axis=-1, eps=1e-05):
    m = jnp.mean(x, axis=axis, keepdims=True)
    v = jnp.var(x, axis=axis, keepdims=True)
    return (x - m) / jnp.sqrt(v + eps)

def _scatter_add(tgt, idx, src, axis=0):
    return tgt.at[idx].add(src)

def _segment_sum(src, seg, n):
    return jax.ops.segment_sum(src, seg, n)
kernel_name = 'mk_adj_resnorm_d4_adj_r2_121148'

def setup_inputs(seed: int=0):
    np.random.seed(seed)
    _w = jnp.asarray

    def _rec_inputs():
        import jax
        import jax.numpy as jnp
        _gk = jax.random.key(seed)
        x = 7.22e-05 + 1 * jax.random.normal(jax.random.fold_in(_gk, 1), (16, 512, 128), jnp.float32)
        _w = (1.0 + jnp.arange(512, dtype=jnp.float32)) ** (-0.5)
        _w = _w / _w.mean()
        _pij = jnp.clip(0.0078125 * _w[:, None] * _w[None, :], 0.0, 1.0)
        _a = jax.random.uniform(jax.random.fold_in(_gk, 2), (512, 512)) < _pij
        _a = jnp.logical_or(_a, jnp.eye(512, dtype=bool))
        adj = _a.astype(jnp.int32)
        return (x, adj)
    x, adj = _rec_inputs()

    def _L0_gnn_setup():
        import jax, jax.numpy as jnp
        import numpy as np
        B, N, D_IN, D_OUT, H = (64, 256, 128, 128, 4)
        HD = D_OUT // H
        key = jax.random.key(seed)
        ks = jax.random.split(key, 10)
        x = jax.random.normal(ks[0], (B, N, D_IN), dtype=jnp.float32)
        adj = jax.random.randint(ks[1], (N, N), 0, 2, dtype=jnp.int32)
        adj = adj.at[jnp.arange(N), jnp.arange(N)].set(1)
        s_in = 1.0 / np.sqrt(D_IN)
        s_out = 1.0 / np.sqrt(D_OUT)
        wq = jax.random.uniform(ks[2], (D_OUT, D_IN), jnp.float32, -s_in, s_in)
        bq = jax.random.uniform(ks[3], (D_OUT,), jnp.float32, -s_in, s_in)
        wk = jax.random.uniform(ks[4], (D_OUT, D_IN), jnp.float32, -s_in, s_in)
        bk = jax.random.uniform(ks[5], (D_OUT,), jnp.float32, -s_in, s_in)
        wv = jax.random.uniform(ks[6], (D_OUT, D_IN), jnp.float32, -s_in, s_in)
        bv = jax.random.uniform(ks[7], (D_OUT,), jnp.float32, -s_in, s_in)
        wo = jax.random.uniform(ks[8], (D_OUT, D_OUT), jnp.float32, -s_out, s_out)
        bo = jax.random.uniform(ks[9], (D_OUT,), jnp.float32, -s_out, s_out)
        return {'x': x, 'adj': adj, 'wq': wq, 'bq': bq, 'wk': wk, 'bk': bk, 'wv': wv, 'bv': bv, 'wo': wo, 'bo': bo}
    _L0_gnn_all = _L0_gnn_setup()
    _L0_gnn_in = {k: v for k, v in _L0_gnn_all.items() if k in ('wq', 'bq', 'wk', 'bk', 'wv', 'bv', 'wo', 'bo')}
    del _L0_gnn_all

    def _L1_gnn_setup():
        import jax, jax.numpy as jnp
        import numpy as np
        B, N, F_IN, F_OUT = (8, 1024, 128, 128)
        key = jax.random.key(seed)
        k1, k2, k3, k4 = jax.random.split(key, 4)
        x = jax.random.normal(k1, (B, N, F_IN), dtype=jnp.float32)
        W = jax.random.normal(k2, (F_IN, F_OUT), dtype=jnp.float32) * (1.0 / np.sqrt(F_IN))
        a = jax.random.normal(k3, (2 * F_OUT, 1), dtype=jnp.float32) * (1.0 / np.sqrt(2 * F_OUT))
        adj = jax.random.randint(k4, (N, N), 0, 2, dtype=jnp.int32)
        return {'x': x, 'W': W, 'a': a, 'adj': adj}
    _L1_gnn_all = _L1_gnn_setup()
    _L1_gnn_in = {k: v for k, v in _L1_gnn_all.items() if k in ('W', 'a')}
    del _L1_gnn_all

    def _L2_gnn_setup():
        import jax, jax.numpy as jnp
        import numpy as np
        ALPHA = 0.2
        EPS = 1e-06
        key = jax.random.key(seed)
        ks = jax.random.split(key, 8)
        B, N, D, H = (2, 1024, 128, 8)
        dh = D // H
        x = jax.random.normal(ks[0], (B, N, D), dtype=jnp.float32)
        adj = jax.random.randint(ks[1], (N, N), 0, 2, dtype=jnp.int32)
        adj = jnp.maximum(adj, jnp.eye(N, dtype=jnp.int32))
        p = jax.random.uniform(ks[2], (B, N, N), dtype=jnp.float32)
        prior = p / jnp.sum(p, axis=-1, keepdims=True)
        W = jax.random.normal(ks[3], (H, D, dh), dtype=jnp.float32) * (1.0 / np.sqrt(D))
        a_src = jax.random.normal(ks[4], (H, dh), dtype=jnp.float32) * (1.0 / np.sqrt(dh))
        a_dst = jax.random.normal(ks[5], (H, dh), dtype=jnp.float32) * (1.0 / np.sqrt(dh))
        beta_tilde = jnp.ones((), dtype=jnp.float32)
        W_out = jax.random.normal(ks[6], (D, D), dtype=jnp.float32) * (1.0 / np.sqrt(D))
        return {'x': x, 'adj': adj, 'prior': prior, 'W': W, 'a_src': a_src, 'a_dst': a_dst, 'beta_tilde': beta_tilde, 'W_out': W_out}
    _L2_gnn_all = _L2_gnn_setup()
    _L2_gnn_in = {k: v for k, v in _L2_gnn_all.items() if k in ('W', 'a_src', 'a_dst', 'beta_tilde', 'W_out')}
    del _L2_gnn_all

    def _L3_gnn_setup():
        import jax, jax.numpy as jnp
        import numpy as np
        ALPHA = 0.2
        NEG_INF = -9000000000000000.0

        def _gat(inp, adj_mask, W, a):
            h = jnp.matmul(inp, W)
            F_ = h.shape[-1]
            f1 = jnp.matmul(h, a[:F_, 0])
            f2 = jnp.matmul(h, a[F_:, 0])
            e = jax.nn.leaky_relu(f1[:, :, None] + f2[:, None, :], ALPHA)
            if adj_mask is not None:
                e = jnp.where(adj_mask[None, :, :] > 0, e, NEG_INF)
            att = jax.nn.softmax(e, axis=2)
            h_prime = jnp.einsum('bij,bjf->bif', att, h)
            return jax.nn.elu(h_prime)
        key = jax.random.key(seed)
        ks = jax.random.split(key, 10)
        B, N, Fin, H, O = (16, 512, 128, 256, 128)

        def xavier(k, shape):
            fan_in, fan_out = (shape[0], shape[-1])
            bound = 1.414 * np.sqrt(6.0 / (fan_in + fan_out))
            return jax.random.uniform(k, shape, jnp.float32, -bound, bound)
        return {'x': jax.random.normal(ks[0], (B, N, Fin), jnp.float32), 'adj': jax.random.randint(ks[1], (N, N), 0, 2, jnp.int32), 'mlp1_w': xavier(ks[2], (Fin, H)), 'mlp1_b': jnp.zeros((H,), jnp.float32), 'mlp2_w': xavier(ks[3], (H, O)), 'mlp2_b': jnp.zeros((O,), jnp.float32), 'W_fc': xavier(ks[4], (H, H)), 'a_fc': xavier(ks[5], (2 * H, 1)), 'W_hand': xavier(ks[6], (O, O)), 'a_hand': xavier(ks[7], (2 * O, 1))}
    _L3_gnn_all = _L3_gnn_setup()
    _L3_gnn_in = {k: v for k, v in _L3_gnn_all.items() if k in ('mlp1_w', 'mlp1_b', 'mlp2_w', 'mlp2_b', 'W_fc', 'a_fc', 'W_hand', 'a_hand')}
    del _L3_gnn_all
    return {'x': x, 'adj': adj, 'L0_gnn_wq': _L0_gnn_in['wq'], 'L0_gnn_bq': _L0_gnn_in['bq'], 'L0_gnn_wk': _L0_gnn_in['wk'], 'L0_gnn_bk': _L0_gnn_in['bk'], 'L0_gnn_wv': _L0_gnn_in['wv'], 'L0_gnn_bv': _L0_gnn_in['bv'], 'L0_gnn_wo': _L0_gnn_in['wo'], 'L0_gnn_bo': _L0_gnn_in['bo'], 'L1_gnn_W': _L1_gnn_in['W'], 'L1_gnn_a': _L1_gnn_in['a'], 'L2_gnn_W': _L2_gnn_in['W'], 'L2_gnn_a_src': _L2_gnn_in['a_src'], 'L2_gnn_a_dst': _L2_gnn_in['a_dst'], 'L2_gnn_beta_tilde': _L2_gnn_in['beta_tilde'], 'L2_gnn_W_out': _L2_gnn_in['W_out'], 'L3_gnn_mlp1_w': _L3_gnn_in['mlp1_w'], 'L3_gnn_mlp1_b': _L3_gnn_in['mlp1_b'], 'L3_gnn_mlp2_w': _L3_gnn_in['mlp2_w'], 'L3_gnn_mlp2_b': _L3_gnn_in['mlp2_b'], 'L3_gnn_W_fc': _L3_gnn_in['W_fc'], 'L3_gnn_a_fc': _L3_gnn_in['a_fc'], 'L3_gnn_W_hand': _L3_gnn_in['W_hand'], 'L3_gnn_a_hand': _L3_gnn_in['a_hand']}

def reference(x, adj, L0_gnn_wq, L0_gnn_bq, L0_gnn_wk, L0_gnn_bk, L0_gnn_wv, L0_gnn_bv, L0_gnn_wo, L0_gnn_bo, L1_gnn_W, L1_gnn_a, L2_gnn_W, L2_gnn_a_src, L2_gnn_a_dst, L2_gnn_beta_tilde, L2_gnn_W_out, L3_gnn_mlp1_w, L3_gnn_mlp1_b, L3_gnn_mlp2_w, L3_gnn_mlp2_b, L3_gnn_W_fc, L3_gnn_a_fc, L3_gnn_W_hand, L3_gnn_a_hand):
    import jax
    import jax.numpy as jnp

    def _L0_gnn_ref(x, adj, wq, bq, wk, bk, wv, bv, wo, bo):
        import jax, jax.numpy as jnp
        import numpy as np
        B, N, D_IN, D_OUT, H = (64, 256, 128, 128, 4)
        HD = D_OUT // H
        b, n, _ = x.shape
        q = (x @ wq.T + bq).reshape(b, n, H, HD).transpose(0, 2, 1, 3)
        k = (x @ wk.T + bk).reshape(b, n, H, HD).transpose(0, 2, 1, 3)
        v = (x @ wv.T + bv).reshape(b, n, H, HD).transpose(0, 2, 1, 3)
        scores = jnp.einsum('bhnd,bhmd->bhnm', q, k) / jnp.sqrt(jnp.float32(HD))
        scores = jnp.where(adj[None, None] == 0, -jnp.inf, scores)
        attn = jnp.nan_to_num(jax.nn.softmax(scores, axis=-1), nan=0.0)
        out = jnp.einsum('bhnm,bhmd->bhnd', attn, v)
        out = out.transpose(0, 2, 1, 3).reshape(b, n, D_OUT)
        return out @ wo.T + bo

    def _L1_gnn_ref(x, W, a, adj):
        import jax, jax.numpy as jnp
        import numpy as np
        B, N, F_IN, F_OUT = (8, 1024, 128, 128)
        h = jnp.einsum('bnf,fo->bno', x, W)
        F = W.shape[1]
        a1 = a[:F, 0]
        a2 = a[F:, 0]
        s1 = jnp.einsum('bno,o->bn', h, a1)
        s2 = jnp.einsum('bno,o->bn', h, a2)
        e = jax.nn.leaky_relu(s1[:, :, None] + s2[:, None, :], negative_slope=0.2)
        mask = adj.astype(h.dtype)[None, :, :]
        e = e + (1.0 - mask) * -1000000000.0
        attention = jax.nn.softmax(e, axis=-1)
        out = jnp.einsum('bnm,bmo->bno', attention, h)
        return out

    def _L2_gnn_ref(x, adj, prior, W, a_src, a_dst, beta_tilde, W_out):
        import jax, jax.numpy as jnp
        import numpy as np
        ALPHA = 0.2
        EPS = 1e-06
        B, N, D = x.shape
        x_proj = jnp.einsum('bnd,hdf->bhnf', x, W)
        e_src = jnp.einsum('bhnf,hf->bhn', x_proj, a_src)
        e_dst = jnp.einsum('bhnf,hf->bhn', x_proj, a_dst)
        e = jax.nn.leaky_relu(e_src[..., :, None] + e_dst[..., None, :], ALPHA)
        beta = jax.nn.softplus(beta_tilde)
        e = e + (beta * jnp.log(prior + EPS))[:, None, :, :]
        neg_inf = jnp.finfo(e.dtype).min
        e = jnp.where(adj[None, None, :, :] > 0, e, neg_inf)
        attn = jax.nn.softmax(e, axis=-1)
        h = jnp.einsum('bhij,bhjf->bhif', attn, x_proj)
        h = h.transpose(0, 2, 1, 3).reshape(B, N, D)
        return h @ W_out.T

    def _L3_gnn_ref(x, adj, mlp1_w, mlp1_b, mlp2_w, mlp2_b, W_fc, a_fc, W_hand, a_hand):
        import jax, jax.numpy as jnp
        import numpy as np
        ALPHA = 0.2
        NEG_INF = -9000000000000000.0

        def _gat(inp, adj_mask, W, a):
            h = jnp.matmul(inp, W)
            F_ = h.shape[-1]
            f1 = jnp.matmul(h, a[:F_, 0])
            f2 = jnp.matmul(h, a[F_:, 0])
            e = jax.nn.leaky_relu(f1[:, :, None] + f2[:, None, :], ALPHA)
            if adj_mask is not None:
                e = jnp.where(adj_mask[None, :, :] > 0, e, NEG_INF)
            att = jax.nn.softmax(e, axis=2)
            h_prime = jnp.einsum('bij,bjf->bif', att, h)
            return jax.nn.elu(h_prime)
        out = jax.nn.relu(jnp.matmul(x, mlp1_w) + mlp1_b)
        residual = out
        out = _gat(jax.nn.relu(out), None, W_fc, a_fc)
        out = jax.nn.elu(out) + residual
        out = jax.nn.relu(jnp.matmul(out, mlp2_w) + mlp2_b)
        residual = out
        out = _gat(jax.nn.relu(out), adj, W_hand, a_hand)
        out = jax.nn.elu(out) + residual
        return jax.nn.relu(out)
    x = _layernorm(x + _L0_gnn_ref(x, adj, L0_gnn_wq, L0_gnn_bq, L0_gnn_wk, L0_gnn_bk, L0_gnn_wv, L0_gnn_bv, L0_gnn_wo, L0_gnn_bo), axis=-1)
    x = _layernorm(x + _L1_gnn_ref(x, L1_gnn_W, L1_gnn_a, adj), axis=-1)
    x = _layernorm(x + _L2_gnn_ref(x, adj, adj[None], L2_gnn_W, L2_gnn_a_src, L2_gnn_a_dst, L2_gnn_beta_tilde, L2_gnn_W_out), axis=-1)
    x = _layernorm(x + _L3_gnn_ref(x, adj, L3_gnn_mlp1_w, L3_gnn_mlp1_b, L3_gnn_mlp2_w, L3_gnn_mlp2_b, L3_gnn_W_fc, L3_gnn_a_fc, L3_gnn_W_hand, L3_gnn_a_hand), axis=-1)
    return x

_drawn_inputs = setup_inputs


def setup_inputs(seed=0):
    import zlib

    import numpy as np

    out = dict(_drawn_inputs(seed))
    spreads = {'L3_gnn_mlp1_b': (0.0, 0.1), 'L3_gnn_mlp2_b': (0.0, 0.1)}
    factors = {'L0_gnn_bq': 8.0, 'L0_gnn_bk': 8.0}
    for name, (base, spread) in spreads.items():
        noise = np.random.default_rng([zlib.crc32(name.encode()), seed]).standard_normal(out[name].shape)
        drawn = base * np.exp(spread * noise) if base else spread * noise
        out[name] = jnp.asarray(drawn.astype(out[name].dtype))
    for name, factor in factors.items():
        out[name] = (out[name] * factor).astype(out[name].dtype)
    return out
```

```python
from contextlib import ExitStack

import concourse.bass as bass
from concourse import mybir

P = 128
N_GRAPHS, N_NODES, D = 16, 512, 128
C = N_NODES // P
HEADS0, DH0 = 4, 32
HEADS2, DH2 = 8, 16
HID = 256
F32, BF16, I32 = mybir.dt.float32, mybir.dt.bfloat16, mybir.dt.int32
ALU = mybir.AluOpType
ACT = mybir.ActivationFunctionType
AX_X = mybir.AxisListType.X
SCALE0 = float(DH0) ** -0.5
MASKED = -1.0e30
LN_EPS = 1e-5
PRIOR_EPS = 1e-6
CAP = -75.0
W2C = 2 * (DH2 + 1)

SCHEDULE = [
    [("l0_s", 0, 1), ("l0_pv", 3, 2), ("l2_s", 7, 4), ("l2_v", 6, 4), ("l0_t", 0, 1), ("l2_g", 0, 3), ("l3_elu", 0, 5),
     ("l0_y", 0, 2), ("l3_zT", 0, 5), ("l3_zT", 1, 5), ("l0_ln", 0, 2), ("l3_m2", 0, 5)],
    [("l0_s", 1, 1), ("l2_s", 0, 3), ("l2_v", 7, 4), ("l3_h2", 0, 5), ("l3_h2", 1, 5), ("l0_nrm", 0, 2), ("l0_t", 1, 1),
     ("l3_sd2", 0, 5), ("l1_xT", 0, 2), ("l2_c", 0, 4), ("l0_r", 0, 1), ("l3_e2", 0, 5), ("l1_h", 0, 2), ("l1_h", 1, 2),
     ("l3_p2", 0, 5)],
    [("l0_s", 2, 1), ("l2_s", 1, 3), ("l2_v", 0, 3), ("l0_pv", 0, 1), ("l1_sd", 0, 2), ("l2_oT", 0, 4), ("l0_t", 2, 1), ("l1_e", 0, 2),
     ("l2_y", 0, 4), ("l3_r", 0, 5), ("l1_p", 0, 2), ("l2_ln", 0, 4), ("x_load", 0, 0)],
    [("l0_s", 3, 1), ("l2_s", 2, 3), ("l2_v", 1, 3), ("l3_o2", 0, 5), ("l3_o2", 1, 5), ("l2_nrm", 0, 4), ("l0_t", 3, 1), ("l0_r", 1, 1),
     ("l3_xT", 0, 4), ("l3_elu2", 0, 5), ("l3_m1", 0, 4), ("l3_m1", 1, 4)],
    [("l0_s", 4, 1), ("l2_s", 3, 3), ("l2_v", 2, 3), ("l0_pv", 1, 1), ("l0_xT", 0, 0), ("l3_h", 0, 4), ("l3_h", 1, 4), ("l3_h", 2, 4),
     ("l3_h", 3, 4), ("l0_t", 4, 1), ("l1_o", 0, 2), ("l1_o", 1, 2), ("l3_f", 0, 5), ("l3_sd", 0, 4), ("l1_ln", 0, 2)],
    [("l0_s", 5, 1), ("l2_s", 4, 3), ("l2_v", 3, 3), ("l0_q", 0, 0), ("l1_nrm", 0, 2), ("l3_e", 0, 4), ("l3_nrm", 0, 5), ("l0_t", 5, 1),
     ("l0_r", 2, 1), ("l0_k", 0, 0), ("l2_xT", 0, 2), ("l3_p", 0, 4), ("l0_v", 0, 0), ("l2_md", 0, 3), ("l2_md", 1, 3)],
    [("l0_s", 6, 1), ("l2_s", 5, 3), ("l2_v", 4, 3), ("l0_pv", 2, 1), ("l2_h", 0, 2), ("l2_h", 1, 2), ("l3_o", 0, 4), ("l3_o", 1, 4),
     ("l0_t", 6, 1), ("l2_dm", 0, 2)],
    [("l0_s", 7, 1), ("l2_s", 6, 3), ("l2_v", 5, 3), ("l2_db", 0, 2), ("l3_o", 2, 4), ("l3_o", 3, 4), ("l0_t", 7, 1),
     ("l2_e", 0, 2), ("l0_r", 3, 1)],
]
ORDER = [entry for slot in SCHEDULE for entry in slot]
LAG = {(name, k): lag for name, k, lag in ORDER}
LAST_LAG = max(LAG.values())
BODIES = N_GRAPHS + LAST_LAG
LOOP_FROM = LAST_LAG + 1 + (LAST_LAG + 1) % 2
LOOP_TO = N_GRAPHS - (N_GRAPHS - LOOP_FROM) % 2

RING_USES = {"l0_xT": 1, "l0_q": 1, "l0_k": 1, "l0_v": 1, "l0_pv": 1, "l0_y": 1,
             "l1_xT": 1, "l1_h": 1, "l1_sd": 2, "l1_o": 1,
             "l2_xT": 1, "l2_h": 1, "l2_dm": 1, "l2_db": 1, "l2_md": 1, "l2_oT": 1, "l2_y": 1,
             "l3_xT": 1, "l3_m1": 1, "l3_h": 1, "l3_sd": 2, "l3_o": 1, "l3_zT": 1, "l3_m2": 1,
             "l3_h2": 1, "l3_r": 1, "l3_sd2": 2, "l3_o2": 1}
RING = 2


class Graph:

    def __init__(self, i, parity, least):
        self.i, self.p, self.least = i, parity % 2, least

    def has(self, back):
        return not isinstance(self.i, int) or self.i >= back

    def back(self, n):
        return Graph(self.i - n, self.p + n, self.least - n)


def ring_counts():
    bank, at = {}, 0
    for name, k, _ in ORDER:
        for u in range(RING_USES.get(name, 0)):
            bank[name, k, u] = at % RING
            at += 1
    used, before = [0] * RING, []
    for t in range(BODIES):
        now = {}
        for name, k, lag in ORDER:
            for u in range(RING_USES.get(name, 0)):
                if 0 <= t - lag < N_GRAPHS:
                    now[name, k, u] = used[bank[name, k, u]]
                    used[bank[name, k, u]] += 1
        before.append(now)
    return bank, before


def build_program(nc, x, adj, w, out):
    bank_of, uses_before = ring_counts()

    with ExitStack() as ctx:
        def sb(name, shape, dt=F32):
            return ctx.enter_context(nc.sbuf_tensor(name, shape, dt))

        def psum(name, shape):
            return ctx.enter_context(nc.psum_tensor(name, shape, F32))

        per_graph = {}

        def sem(name, n=0):
            s = ctx.enter_context(nc.semaphore(name))
            per_graph[name] = n
            named[name] = s
            return s

        named = {}

        ident = sb("ident", [P, P])
        ident_b = sb("ident_b", [P, P], BF16)
        ones = sb("ones", [P, P])
        neg_half = sb("neg_half", [P, C])
        mask_add = sb("mask_add", [P, C, N_NODES], BF16)
        mask_t = sb("mask_t", [P, C, N_NODES], BF16)
        wT = {n: sb(n + "T", [P, D]) for n in ("wq", "wk", "wv", "wo", "w_out")}
        bias_q, bias_k = sb("bias_q", [P, 1]), sb("bias_k", [P, 1])
        bias_v, bias_o = sb("bias_v", [P, D]), sb("bias_o", [P, D])
        w1_cat = sb("w1_cat", [P, 2 + D])
        w2_cat = sb("w2_cat", [P, D + 2 * HEADS2])
        w3a = sb("w3a", [P, HID])
        b3a = sb("b3a", [P, 2])
        w3_fc = sb("w3_fc", [P, 2, 2 + HID])
        w3b = sb("w3b", [P, 2, D])
        b3b = sb("b3b", [P, 1])
        w3_hand = sb("w3_hand", [P, 2 + D])
        ln_prior = sb("ln_prior", [P, 1])
        pre = sb("pre", [P, 8])
        neg_one = sb("neg_one", [P, 1])
        waited = sb("waited", [P, 1])
        ln_eps = sb("ln_eps", [P, C])

        x_in = [sb(f"x_in{q}", [P, C, D]) for q in range(2)]
        x1 = [sb(f"x1_{q}", [P, C, D]) for q in range(2)]
        x2 = [sb(f"x2_{q}", [P, C, D]) for q in range(2)]
        x3 = [sb(f"x3_{q}", [P, C, D]) for q in range(2)]
        xT = {n: sb("xT" + n, [P, N_NODES]) for n in ("l0", "l1", "l2", "l3")}
        piece = {n: sb("piece_" + n, [P, 3, N_NODES], BF16) for n in "qk"}
        rest = sb("rest", [P, N_NODES])
        stack = {n: [[sb(f"stack_{n}{g}_{q}", [P, HEADS0, N_NODES], BF16) for g in range(2)] for q in range(2)]
                 for n in "qk"}
        v0 = [sb(f"v0_{q}", [P, C, D]) for q in range(2)]
        row_max = sb("row_max", [P, 16])
        neg_max = sb("neg_max", [P, 16])
        probs = sb("probs", [P, 2, N_NODES])
        den0 = sb("den0", [P, 16])
        rden0 = sb("rden0", [P, HEADS0, DH0])
        probs_t = sb("probs_t", [P, HEADS0, C, P])
        rden_t = sb("rden_t", [P, P])
        o0_t = sb("o0_t", [P, N_NODES])
        stats = {n: sb("stats_" + n, [P, C, 6]) for n in ("l0", "l1", "l2", "l3")}
        mv = {n: sb("mv_" + n, [P, C, 2]) for n in ("l0", "l1", "l2", "l3")}
        rstd = {n: sb("rstd_" + n, [P, C]) for n in ("l0", "l1", "l2", "l3")}
        t1 = sb("t1", [P, C, D + 4])
        t3 = sb("t3", [P, C, HID + 4])
        t4 = sb("t4", [P, C, D + 4])
        gat = {}
        for n in ("l1", "l3", "l3b"):
            gat[n] = dict(ndmax=sb(n + "_ndmax", [P, 1]), dd=sb(n + "_dd", [P, C]), b=sb(n + "_b", [P, C]),
                          g=sb(n + "_g", [P, C]), R=sb(n + "_R", [P, N_NODES]),
                          P=sb(n + "_P", [P, C, N_NODES]), rden=sb(n + "_rden", [P, C]))
        t2 = [sb(f"t2_{q}", [P, C, D + 2 * HEADS2]) for q in range(2)]
        dmax8 = sb("dmax8", [HEADS2, 1])
        dmax_diag = sb("dmax_diag", [HEADS2, HEADS2])
        dmax_all = sb("dmax_all", [P, HEADS2])
        small2 = sb("small2", [P, 2, C, HEADS2])
        neg_d = [sb(f"neg_d{q}", [P, C, HEADS2]) for q in range(2)]
        R2 = [sb(f"R2_{q}", [P, C, HEADS2]) for q in range(2)]
        bg2 = sb("bg2", [P, 2, C, HEADS2])
        G = sb("G", [P, C * HEADS2, W2C])
        GS = [sb(f"GS{q}", [P, C * HEADS2, 3, W2C], BF16) for q in range(2)]
        B1 = [sb(f"B1_{q}", [P, C, N_NODES], BF16) for q in range(2)]
        EV = [sb(f"EV{q}", [P, C, 3, W2C]) for q in range(2)]
        U = sb("U", [P, HEADS2, C, W2C])
        MD = sb("MD", [P, C, HEADS2 * (DH2 + 1)])
        rden2 = sb("rden2", [P, C, HEADS2])
        O2 = sb("O2", [P, C, D])
        O2_t = sb("O2_t", [P, N_NODES])
        h3_t = sb("h3_t", [P, 2, N_NODES])
        v3 = sb("v3", [P, C, HID])
        e3 = sb("e3", [P, C, HID])
        out2_t = sb("out2_t", [P, N_NODES])
        out2 = sb("out2", [P, C, D])
        v4 = sb("v4", [P, C, D])
        e4 = sb("e4", [P, C, D])
        x4 = [v4, v4]

        ps_s = psum("ps_s", [P, 2, N_NODES])
        ps_t = psum("ps_t", [P, 2, N_NODES])
        ps_b = psum("ps_b", [P, N_NODES])
        ps_v = psum("ps_v", [P, N_NODES])
        ring = [psum(f"ring{k}", [P, N_NODES]) for k in range(RING)]

        sem("l3_sum", 1)
        s_w = sem("weights_loaded")
        s_adj = sem("adj_loaded")
        s_const = sem("consts_made")
        s_pre_pe = sem("setup_pe")
        s_pre_dve = sem("setup_dve")
        s_pre_act = sem("setup_act")
        s_setup = sem("setup_done")
        fold_sem = sem("folded")
        ring_written = [sem(f"ring_written{k}") for k in range(RING)]
        ring_read = [sem(f"ring_read{k}") for k in range(RING)]
        for name, n in [("x_loaded", 16), ("x_biased", 1), ("q_high", 1), ("k_high", 1), ("q_mid", 1), ("k_mid", 1),
                        ("q_split", 1), ("k_split", 1), ("q_spilled", 16), ("k_spilled", 16),
                        ("q_stacked", 128), ("k_stacked", 128),
                        ("s0_made", 8), ("max0", 8), ("neg_max0", 8), ("exp0", 16), ("t0_made", 8), ("t0_out", 8),
                        ("den0_safe", 4), ("rden0_made", 4), ("rden0_out", 4),
                        ("b1_made", 8), ("s2_made", 8), ("v2_made", 8), ("v2_out", 8), ("u2_made", 16),
                        ("dmax8_diag", 1), ("small2_made", 2), ("exp2", 3), ("g2_made", 4), ("gh2", 1),
                        ("gr2", 1), ("gm2", 1), ("gl2", 1), ("c2", 3), ("rden2_made", 1), ("o2_made", 1),
                        ("u3_made", 1), ("e3_first", 1), ("e3_made", 1), ("z3_made", 1),
                        ("u4_made", 1), ("e4_first", 1), ("e4_made", 1), ("z4", 2), ("stored", 16)]:
            sem(name, n)
        for n in ("l0", "l1", "l2", "l3"):
            sem(n + "_stats", 1)
            sem(n + "_mv", 1)
            sem(n + "_var", 1)
            sem(n + "_rstd", 1)
            sem(n + "_x", 1)
        for n in ("l1", "l3", "l3b"):
            sem(n + "_dd", 1)
            sem(n + "_b", 2)
            sem(n + "_R", 1)
            sem(n + "_P", 4)
            sem(n + "_Pm", 4)
            sem(n + "_rden", 4 if n == "l3" else 2)

        def wait(eng, name, g, k, back=0):
            if g.has(back):
                v = per_graph[name] * (g.i - back) + k
                assert isinstance(v, int) or per_graph[name] * (g.least - back) + k >= 1, (name, back, k)
                if not isinstance(v, int) or v > 0:
                    eng.wait_ge(named[name], v)

        def uses(stage, g, k, u):
            t = g.i + LAG[stage, k]
            key = (stage, k, u)
            if isinstance(t, int):
                return uses_before[t][key]
            assert g.least + LAG[stage, k] >= LOOP_FROM - 1, key
            step = uses_before[LOOP_FROM + 1][key] - uses_before[LOOP_FROM][key]
            return (t - LOOP_FROM) * step + uses_before[LOOP_FROM][key]

        def written(eng, stage, g, k=0, u=0, back=0):
            if g.has(back):
                eng.wait_ge(ring_written[bank_of[stage, k, u]], uses(stage, g.back(back), k, u) + 1)

        def drained(eng, stage, g, k=0, u=0, back=0):
            if g.has(back):
                eng.wait_ge(ring_read[bank_of[stage, k, u]], uses(stage, g.back(back), k, u) + 1)

        def free_bank(eng, stage, g, k=0, u=0):
            n = uses(stage, g, k, u)
            b = bank_of[stage, k, u]
            if not isinstance(n, int) or n > 0:
                eng.wait_ge(ring_read[b], n)
            return ring[b]

        def bank(stage, k=0, u=0):
            return ring[bank_of[stage, k, u]]

        def put(ins, stage, k=0, u=0):
            ins.then_inc(ring_written[bank_of[stage, k, u]], 1)

        def got(ins, stage, k=0, u=0):
            ins.then_inc(ring_read[bank_of[stage, k, u]], 1)

        def done(ins, name):
            ins.then_inc(named[name], 1)

        def run_bodies(eng, stages):
            def body(t, parity, known):
                for name, k, lag in ORDER:
                    if name in stages and (known is None or 0 <= known - lag < N_GRAPHS):
                        stages[name](Graph(t - lag, parity - lag, LOOP_FROM + parity % 2 - lag if known is None else known - lag), k)
            for t in range(LOOP_FROM):
                body(t, t, t)
            with eng.Fori(LOOP_FROM, LOOP_TO - 1, 2) as t:
                body(t, 0, None)
                body(t + 1, 1, None)
            for t in range(LOOP_TO, BODIES):
                body(t, t, t)

        spill = {n: nc.dram_tensor("spill_" + n, [P, 3, N_NODES], BF16, kind="Internal").ap() for n in "qk"}
        x_v = x.rearrange("b (p c) d -> b p c d", c=C)
        out_v = out.rearrange("b (p c) d -> b p c d", c=C)
        adj_i = gat["l1"]["P"][:, :, :].bitcast(I32)
        adj_m = gat["l3"]["P"]
        raw = gat["l3b"]["P"]
        RAW = {"wq": 0, "wk": 1, "wv": 2, "wo": 3, "w_out": 4}
        fold = probs_t
        foldv = fold[:, :, :, :].rearrange("p a b c -> p (a b c)")

        block = ctx.enter_context(nc.Block())

        N_WEIGHT_DMAS = 24


        @block.sync
        def _(sp):
            sp.dma_start(adj_i, adj.rearrange("(p c) n -> p c n", c=C)).then_inc(s_adj, 16)
            rawf = raw[:, :, :].rearrange("p a b -> p (a b)")

            def load(dst, src):
                sp.dma_start(dst, src).then_inc(s_w, 16)

            def everywhere(vec, n):
                return vec.rearrange("(o n) -> o n", o=1).broadcast_to([P, n])

            for n, key in (("wq", "L0_gnn_wq"), ("wk", "L0_gnn_wk"), ("wv", "L0_gnn_wv"), ("wo", "L0_gnn_wo"),
                           ("w_out", "L2_gnn_W_out")):
                load(rawf[:, RAW[n] * D:(RAW[n] + 1) * D], w[key])
            load(bias_q[:, :], w["L0_gnn_bq"].rearrange("(p o) -> p o", o=1))
            load(bias_k[:, :], w["L0_gnn_bk"].rearrange("(p o) -> p o", o=1))
            load(bias_v[:, :], everywhere(w["L0_gnn_bv"], D))
            load(bias_o[:, :], everywhere(w["L0_gnn_bo"], D))
            load(w1_cat[:, 2:2 + D], w["L1_gnn_W"])
            load(w2_cat[:, 0:D].rearrange("p (h o) -> p h o", h=HEADS2), w["L2_gnn_W"].rearrange("h d o -> d h o"))
            load(w3a[:, :], w["L3_gnn_mlp1_w"])
            for q in range(2):
                load(b3a[:, q:q + 1], w["L3_gnn_mlp1_b"].rearrange("(k p o) -> k p o", p=P, o=1)[q])
            load(w3_fc[:, :, 2:2 + HID], w["L3_gnn_W_fc"].rearrange("(k p) n -> p k n", p=P))
            load(w3b[:, :, :], w["L3_gnn_mlp2_w"].rearrange("(k p) n -> p k n", p=P))
            load(b3b[:, :], w["L3_gnn_mlp2_b"].rearrange("(p o) -> p o", o=1))
            load(w3_hand[:, 2:2 + D], w["L3_gnn_W_hand"])
            load(foldv[:, 0:256], everywhere(w["L1_gnn_a"].rearrange("a o -> (a o)"), 256))
            load(foldv[:, 256:384], everywhere(w["L2_gnn_a_src"].rearrange("a o -> (a o)"), 128))
            load(foldv[:, 384:512], everywhere(w["L2_gnn_a_dst"].rearrange("a o -> (a o)"), 128))
            load(foldv[:, 512:1024], everywhere(w["L3_gnn_a_fc"].rearrange("a o -> (a o)"), 512))
            load(foldv[:, 1024:1280], everywhere(w["L3_gnn_a_hand"].rearrange("a o -> (a o)"), 256))
            load(pre[:, 0:1], w["L2_gnn_beta_tilde"].rearrange("(o n) -> o n", o=1).broadcast_to([P, 1]))

            def x_load(g, k):
                wait(sp, "l0_stats", g, 1, back=2)
                sp.dma_start(x_in[g.p][:, :, :], x_v[g.i]).then_inc(named["x_loaded"], 16)

            def split(n, g):
                wait(sp, n + "_split", g, 1)
                wait(sp, n + "_stacked", g, 128, back=1)
                sp.dma_start(spill[n], piece[n][:, :, :]).then_inc(named[n + "_spilled"], 16)
                wait(sp, "s0_made", g, 8, back=2)
                wait(sp, n + "_spilled", g, 16)
                parts = {"q": ((0, 0, 1, 1), (0, 2, 1, 2)), "k": ((0, 1, 0, 1), (2, 0, 2, 1))}[n]
                for q in range(2):
                    for blk in range(4):
                        sp.dma_start(stack[n][q][g.p][DH0 * blk:DH0 * (blk + 1), :, :],
                                     spill[n].rearrange("(h r) s n -> s r h n", h=HEADS0)[parts[q][blk]])\
                          .then_inc(named[n + "_stacked"], 16)

            def store(g, k):
                wait(sp, "l3_x", g, 1)
                sp.dma_start(out_v[g.i], x4[g.p][:, :, :]).then_inc(named["stored"], 16)

            run_bodies(sp, {"x_load": x_load, "l0_q": lambda g, k: split("q", g),
                            "l0_k": lambda g, k: split("k", g), "l3_nrm": store})
            sp.wait_ge(named["stored"], 16 * N_GRAPHS)

        @block.tensor
        def _(pe):
            pe.wait_ge(s_const, 4)
            pe.wait_ge(s_w, 16 * N_WEIGHT_DMAS)
            rawf = raw[:, :, :].rearrange("p a b -> p (a b)")
            for n in ("wq", "wk", "wv", "wo"):
                last = pe.transpose(ring[0][:, RAW[n] * D:(RAW[n] + 1) * D], rawf[:, RAW[n] * D:(RAW[n] + 1) * D], ident[:, :])
            last = pe.transpose(ring[1][:, 0:D], rawf[:, 4 * D:5 * D], ident[:, :])
            last.then_inc(s_pre_pe, 1)
            pe.wait_ge(s_pre_dve, 2)
            for j in range(C):
                pe.wait_ge(s_pre_act, j + 1)
                for c in range(C):
                    last = pe.transpose(ring[0][:, c * P:(c + 1) * P], adj_m[:, c, j * P:(j + 1) * P], ident[:, :])
                last.then_inc(s_pre_pe, 1)
            pe.wait_ge(s_setup, 2)

            def to_T(stage, src, ready):
                def f(g, k):
                    ready(g)
                    ps = free_bank(pe, stage, g)
                    for c in range(C):
                        last = pe.transpose(ps[:, c * P:(c + 1) * P], src(g)[:, c, :], ident[:, :])
                    put(last, stage)
                return f

            def l0_qk(n):
                def f(g, k):
                    drained(pe, "l0_xT", g)
                    ps = free_bank(pe, "l0_" + n, g)
                    put(pe.matmul(ps[:, :], wT["w" + n][:, :], xT["l0"][:, :], start=True, stop=True), "l0_" + n)
                return f

            def l0_v(g, k):
                drained(pe, "l0_xT", g)
                ps = free_bank(pe, "l0_v", g)
                for c in range(C):
                    last = pe.matmul(ps[:, c * D:(c + 1) * D], xT["l0"][:, c * P:(c + 1) * P], wT["wv"][:, :],
                                     start=True, stop=True)
                put(last, "l0_v")

            def l0_s(g, s):
                c, h0 = s // 2, 2 * (s % 2)
                if s == 0:
                    wait(pe, "q_stacked", g, 128)
                    wait(pe, "k_stacked", g, 128)
                wait(pe, "exp0", g, 2 * s)
                for h in range(2):
                    for q in range(2):
                        pe.matmul(ps_s[:, h, :], stack["q"][q][g.p][:, h0 + h, c * P:(c + 1) * P],
                                  stack["k"][q][g.p][:, h0 + h, :], start=(q == 0), stop=False)
                    last = pe.matmul(ps_s[:, h, :], ident_b[:, :], mask_add[:, c, :], start=False, stop=True)
                done(last, "s0_made")

            def l0_t(g, s):
                wait(pe, "exp0", g, 2 * s + 2)
                wait(pe, "t0_out", g, s)
                for h in range(2):
                    for j in range(C):
                        last = pe.transpose(ps_t[:, h, j * P:(j + 1) * P], probs[:, h, j * P:(j + 1) * P], ident[:, :])
                done(last, "t0_made")

            def l0_pv(g, c):
                wait(pe, "t0_out", g, 2 * c + 2)
                if c == 0:
                    drained(pe, "l0_v", g)
                wait(pe, "rden0_made", g, c + 1)
                ps = free_bank(pe, "l0_pv", g, c)
                for j in range(C):
                    for h in range(HEADS0):
                        pe.matmul(ps[DH0 * h:DH0 * (h + 1), 0:P], v0[g.p][:, j, DH0 * h:DH0 * (h + 1)],
                                  probs_t[:, h, j, :], start=(j == 0), stop=(j == C - 1))
                put(pe.transpose(ps[:, P:2 * P],
                                 rden0[:, :, :].rearrange("p h o -> p (h o)"),
                                 ident[:, :]), "l0_pv", c)

            def l0_y(g, k):
                drained(pe, "l0_pv", g, 3)
                ps = free_bank(pe, "l0_y", g)
                for c in range(C):
                    last = pe.matmul(ps[:, c * D:(c + 1) * D], o0_t[:, c * P:(c + 1) * P], wT["wo"][:, :],
                                     start=True, stop=True)
                put(last, "l0_y")

            def project(stage, src, src_ready, cat, width):
                def f(g, k):
                    src_ready(g)
                    ps = free_bank(pe, stage, g, k)
                    for c in range(2):
                        last = pe.matmul(ps[:, c * width:(c + 1) * width], src[:, (2 * k + c) * P:(2 * k + c + 1) * P],
                                         cat[:, 0:width], start=True, stop=True)
                    put(last, stage, k)
                return f

            def spread(stage, t, ready):
                def f(g, k):
                    ready(g)
                    for u, col in ((0, 1), (1, 0)):
                        ps = free_bank(pe, stage, g, 0, u)
                        for c in range(C):
                            last = pe.transpose(ps[:, c * P:(c + 1) * P], t[:, c, col:col + 1].broadcast_to([P, P]),
                                                ident[:, :])
                        put(last, stage, 0, u)
                return f

            def attend(stage, n, t, masked):
                def f(g, k):
                    if k == 0:
                        wait(pe, n + ("_Pm" if masked else "_P"), g, 4)
                    ps = free_bank(pe, stage, g, k)
                    for c in range(2):
                        for j in range(C):
                            last = pe.matmul(ps[:, c * (D + 1):(c + 1) * (D + 1)],
                                             gat[n]["P"][:, j, (2 * k + c) * P:(2 * k + c + 1) * P],
                                             t[:, j, 2:3 + D], start=(j == 0), stop=(j == C - 1))
                    put(last, stage, k)
                return f

            def l2_dm(g, k):
                drained(pe, "l2_h", g, 0)
                drained(pe, "l2_h", g, 1)
                ps = free_bank(pe, "l2_dm", g)
                for c in range(C):
                    last = pe.transpose(ps[0:HEADS2, c * P:(c + 1) * P], t2[g.p][:, c, D + HEADS2:D + 2 * HEADS2],
                                        ident[:, :])
                put(last, "l2_dm")

            def l2_db(g, k):
                wait(pe, "dmax8_diag", g, 1)
                ps = free_bank(pe, "l2_db", g)
                put(pe.matmul(ps[:, 0:HEADS2], ones[0:HEADS2, :], dmax_diag[:, :], start=True, stop=True), "l2_db")

            def l2_s(g, h):
                wait(pe, "b1_made", g, h)
                for c in range(C):
                    last = pe.transpose(ps_b[:, c * P:(c + 1) * P],
                                        t2[g.p][:, c, D + h:D + h + 1].broadcast_to([P, P]), ident[:, :])
                done(last, "s2_made")

            def l2_v(g, h):
                wait(pe, "b1_made", g, h + 1)
                if h == 0:
                    wait(pe, "gl2", g, 1)
                wait(pe, "v2_out", g, h)
                w3 = 3 * W2C
                for c in range(C):
                    for j in range(C):
                        last = pe.matmul(ps_v[:, c * w3:(c + 1) * w3], B1[h % 2][:, j, c * P:(c + 1) * P],
                                         GS[g.p][:, j * HEADS2 + h, :, :].rearrange("p a b -> p (a b)"),
                                         start=(j == 0), stop=(j == C - 1))
                done(last, "v2_made")

            def l2_md(g, k):
                wait(pe, "gl2", g, 1)
                ps = free_bank(pe, "l2_md", g, k)
                wd = HEADS2 * (DH2 + 1)
                for c in range(2):
                    for j in range(C):
                        for q in range(3):
                            last = pe.matmul(ps[:, c * wd:(c + 1) * wd], mask_t[:, j, (2 * k + c) * P:(2 * k + c + 1) * P],
                                             GS[g.p][:, j * HEADS2:(j + 1) * HEADS2, q, DH2 + 1:W2C],
                                             start=(j == 0 and q == 0), stop=(j == C - 1 and q == 2))
                put(last, "l2_md", k)

            def l2_y(g, k):
                drained(pe, "l2_oT", g)
                ps = free_bank(pe, "l2_y", g)
                for c in range(C):
                    last = pe.matmul(ps[:, c * D:(c + 1) * D], O2_t[:, c * P:(c + 1) * P], wT["w_out"][:, :],
                                     start=True, stop=True)
                put(last, "l2_y")

            def l3_m1(g, k):
                drained(pe, "l3_xT", g)
                ps = free_bank(pe, "l3_m1", g, k)
                put(pe.matmul(ps[:, :], w3a[:, k * P:(k + 1) * P], xT["l3"][:, :], start=True, stop=True), "l3_m1", k)

            def l3_h(g, c):
                drained(pe, "l3_m1", g, 0)
                drained(pe, "l3_m1", g, 1)
                ps = free_bank(pe, "l3_h", g, c)
                for q in range(2):
                    last = pe.matmul(ps[:, 0:2 + HID], h3_t[:, q, c * P:(c + 1) * P], w3_fc[:, q, :],
                                     start=(q == 0), stop=(q == 1))
                put(last, "l3_h", c)

            def l3_o(g, c):
                wait(pe, "l3_P", g, 4)
                ps = free_bank(pe, "l3_o", g, c)
                for j in range(C):
                    last = pe.matmul(ps[:, 0:HID + 1], gat["l3"]["P"][:, j, c * P:(c + 1) * P], t3[:, j, 2:3 + HID],
                                     start=(j == 0), stop=(j == C - 1))
                put(last, "l3_o", c)

            def l3_zT(g, k):
                wait(pe, "z3_made", g, 1)
                ps = free_bank(pe, "l3_zT", g, k)
                for c in range(C):
                    last = pe.transpose(ps[:, c * P:(c + 1) * P], v3[:, c, k * P:(k + 1) * P], ident[:, :])
                put(last, "l3_zT", k)

            def l3_m2(g, k):
                drained(pe, "l3_zT", g, 0)
                drained(pe, "l3_zT", g, 1)
                ps = free_bank(pe, "l3_m2", g)
                for q in range(2):
                    last = pe.matmul(ps[:, :], w3b[:, q, :], h3_t[:, q, :], start=(q == 0), stop=(q == 1))
                put(last, "l3_m2")

            def l3_r(g, k):
                drained(pe, "l3_m2", g)
                ps = free_bank(pe, "l3_r", g)
                for c in range(C):
                    last = pe.transpose(ps[:, c * P:(c + 1) * P], out2_t[:, c * P:(c + 1) * P], ident[:, :])
                put(last, "l3_r")

            def both(stage):
                def f(g):
                    drained(pe, stage, g, 0)
                    drained(pe, stage, g, 1)
                return f

            def all4(stage):
                def f(g):
                    for c in range(C):
                        drained(pe, stage, g, c)
                return f

            run_bodies(pe, {
                "l0_xT": to_T("l0_xT", lambda g: x_in[g.p], lambda g: wait(pe, "x_loaded", g, 16)),
                "l0_q": l0_qk("q"), "l0_k": l0_qk("k"), "l0_v": l0_v, "l0_s": l0_s, "l0_t": l0_t, "l0_pv": l0_pv, "l0_y": l0_y,
                "l1_xT": to_T("l1_xT", lambda g: x1[g.p], lambda g: wait(pe, "l0_x", g, 1)),
                "l1_h": project("l1_h", xT["l1"], lambda g: drained(pe, "l1_xT", g), w1_cat, D + 2),
                "l1_sd": spread("l1_sd", t1, both("l1_h")),
                "l1_o": attend("l1_o", "l1", t1, True),
                "l2_xT": to_T("l2_xT", lambda g: x2[g.p], lambda g: wait(pe, "l1_x", g, 1)),
                "l2_h": project("l2_h", xT["l2"], lambda g: drained(pe, "l2_xT", g), w2_cat, D + 2 * HEADS2),
                "l2_dm": l2_dm, "l2_db": l2_db, "l2_s": l2_s, "l2_v": l2_v, "l2_md": l2_md,
                "l2_oT": to_T("l2_oT", lambda g: O2, lambda g: wait(pe, "o2_made", g, 1)),
                "l2_y": l2_y,
                "l3_xT": to_T("l3_xT", lambda g: x3[g.p], lambda g: wait(pe, "l2_x", g, 1)),
                "l3_m1": l3_m1, "l3_h": l3_h, "l3_sd": spread("l3_sd", t3, all4("l3_h")), "l3_o": l3_o,
                "l3_zT": l3_zT, "l3_m2": l3_m2,
                "l3_h2": project("l3_h2", out2_t, lambda g: drained(pe, "l3_m2", g), w3_hand, D + 2),
                "l3_r": l3_r, "l3_sd2": spread("l3_sd2", t4, both("l3_h2")),
                "l3_o2": attend("l3_o2", "l3b", t4, True),
            })

        @block.scalar
        def _(act):
            act.preload_act_table_set("natural_log_exp_and_others")
            act.wait_ge(s_pre_pe, 1)
            for n in ("wq", "wk", "wv", "wo"):
                last = act.activation(wT[n][:, :], ring[0][:, RAW[n] * D:(RAW[n] + 1) * D], ACT.Copy)
            last.then_inc(s_pre_act, 1)
            act.activation(wT["w_out"][:, :], ring[1][:, 0:D], ACT.Copy)
            for j in range(C):
                act.wait_ge(s_pre_pe, j + 2)
                act.activation(mask_t[:, j, :], ring[0][:, :], ACT.Copy).then_inc(s_pre_act, 1)
            act.wait_ge(s_pre_dve, 4)
            act.activation(pre[:, 3:4], pre[:, 2:3], ACT.Exp).then_inc(s_pre_act, 1)
            act.wait_ge(s_pre_act, 6)
            act.activation(pre[:, 4:5], pre[:, 3:4], ACT.Ln, bias=1.0)
            act.activation(pre[:, 5:6], ones[:, 0:1], ACT.Ln, bias=pre[:, 6:7]).then_inc(s_setup, 1)
            act.wait_ge(s_setup, 2)

            def xT_out(stage, n, reader, rk):
                def f(g, k):
                    written(act, stage, g)
                    written(act, reader, g, rk, back=1)
                    got(act.activation(xT[n][:, :], bank(stage)[:, :], ACT.Copy), stage)
                return f

            def l0_qk(n, bias):
                def f(g, k):
                    written(act, "l0_" + n, g)
                    wait(act, n + "_spilled", g, 16, back=1)
                    done(act.activation(piece[n][:, 0, :], bank("l0_" + n)[:, :], ACT.Identity, bias=bias[:, 0:1]),
                         n + "_high")
                return f

            def l0_s(g, s):
                wait(act, "neg_max0", g, s + 1)
                wait(act, "t0_made", g, s)
                wait(act, "rden0_made", g, 4, back=1)
                for h in range(2):
                    done(act.activation(probs[:, h, :], ps_s[:, h, :], ACT.Exp, bias=neg_max[:, 2 * s + h:2 * s + h + 1],
                                        scale=SCALE0, accum_out=den0[:, 2 * s + h:2 * s + h + 1]), "exp0")

            def l0_t(g, s):
                c, h0 = s // 2, 2 * (s % 2)
                wait(act, "t0_made", g, s + 1)
                if c:
                    written(act, "l0_pv", g, c - 1)
                else:
                    written(act, "l0_pv", g, C - 1, back=1)
                done(act.activation(probs_t[:, h0:h0 + 2, :, :].rearrange("p h j n -> p (h j n)"),
                                    ps_t[:, :, :].rearrange("p h n -> p (h n)"), ACT.Copy), "t0_out")

            def l0_pv(g, c):
                written(act, "l0_pv", g, c)
                if c:
                    drained(act, "l0_pv", g, c - 1)
                else:
                    drained(act, "l0_pv", g, C - 1, back=1)
                done(act.activation(rden_t[:, :], bank("l0_pv", c)[:, P:2 * P], ACT.Copy), "rden0_out")

            def h_out(stage, t, width, n_free):
                def f(g, k):
                    written(act, stage, g, k)
                    n_free(g)
                    tt = t(g)
                    got(act.activation(tt[:, 2 * k:2 * k + 2, 0:width],
                                       bank(stage, k)[:, 0:2 * width].rearrange("p (c n) -> p c n", c=2), ACT.Copy), stage, k)
                return f

            def gat_exp(n):
                def f(g, k):
                    wait(act, n + "_dd", g, 1)
                    wait(act, n + "_P", g, 4, back=1)
                    t = gat[n]
                    done(act.activation(t["b"][:, :], t["dd"][:, :], ACT.Exp), n + "_b")
                    done(act.activation(t["g"][:, :], t["dd"][:, :], ACT.Exp, scale=0.2), n + "_b")
                    drained(act, {"l1": "l1_sd", "l3": "l3_sd", "l3b": "l3_sd2"}[n], g, 0, 1)
                    done(act.activation(t["R"][:, :], t["R"][:, :], ACT.Exp, scale=-0.8), n + "_R")
                return f

            def l2_e(g, k):
                wait(act, "small2_made", g, 2)
                wait(act, "g2_made", g, 4, back=1)
                done(act.activation(bg2[:, 0, :, :], small2[:, 0, :, :], ACT.Exp, bias=ln_prior[:, 0:1]), "exp2")
                done(act.activation(bg2[:, 1, :, :], small2[:, 0, :, :], ACT.Exp, bias=ln_prior[:, 0:1], scale=0.2), "exp2")
                wait(act, "c2", g, 3, back=2)
                done(act.activation(R2[g.p][:, :, :], small2[:, 1, :, :], ACT.Exp, scale=-0.8), "exp2")

            def l2_g(g, k):
                wait(act, "g2_made", g, 4)
                wait(act, "v2_made", g, 8, back=2)
                wait(act, "c2", g, 3, back=2)
                done(act.activation(GS[g.p][:, :, 0, :], G[:, :, :], ACT.Copy), "gh2")

            def l2_v(g, h):
                wait(act, "v2_made", g, h + 1)
                wait(act, "u2_made", g, 2 * h - 2)
                done(act.activation(EV[h % 2][:, :, :, :].rearrange("p c q n -> p (c q n)"), ps_v[:, 0:C * 3 * W2C], ACT.Copy),
                     "v2_out")

            def l2_md(g, k):
                written(act, "l2_md", g, k)
                wait(act, "c2", g, 1, back=1)
                wd = HEADS2 * (DH2 + 1)
                got(act.activation(MD[:, 2 * k:2 * k + 2, :], bank("l2_md", k)[:, 0:2 * wd].rearrange("p (c n) -> p c n", c=2),
                                   ACT.Copy), "l2_md", k)

            def l2_oT(g, k):
                written(act, "l2_oT", g)
                written(act, "l2_y", g, back=1)
                got(act.activation(O2_t[:, :], bank("l2_oT")[:, :], ACT.Copy), "l2_oT")

            def l3_m1(g, k):
                written(act, "l3_m1", g, k)
                written(act, "l3_m2", g, back=1)
                got(act.activation(h3_t[:, k, :], bank("l3_m1", k)[:, :], ACT.Relu, bias=b3a[:, k:k + 1]), "l3_m1", k)

            def l3_h(g, c):
                written(act, "l3_h", g, c)
                written(act, "l3_o", g, C - 1, back=1)
                got(act.activation(t3[:, c, 0:2 + HID], bank("l3_h", c)[:, 0:2 + HID], ACT.Copy), "l3_h", c)

            def elu(n, tile):
                def f(g, k):
                    wait(act, f"u{n}_made", g, 1)
                    done(act.activation(tile[:, :, :], tile[:, :, :], ACT.Exp), f"e{n}_first")
                    wait(act, f"e{n}_first", g, 1)
                    done(act.activation(tile[:, :, :], tile[:, :, :], ACT.Exp, bias=neg_one[:, 0:1]), f"e{n}_made")
                return f

            def l3_m2(g, k):
                written(act, "l3_m2", g)
                written(act, "l3_r", g, back=1)
                written(act, "l3_h2", g, 1, back=1)
                got(act.activation(out2_t[:, :], bank("l3_m2")[:, :], ACT.Relu, bias=b3b[:, 0:1]), "l3_m2")

            def l3_r(g, k):
                written(act, "l3_r", g)
                wait(act, "z4", g, 2, back=1)
                got(act.activation(out2[:, :, :].rearrange("p c n -> p (c n)"), bank("l3_r")[:, :], ACT.Copy), "l3_r")

            run_bodies(act, {
                "l0_xT": xT_out("l0_xT", "l0", "l0_v", 0), "l0_q": l0_qk("q", bias_q), "l0_k": l0_qk("k", bias_k),
                "l0_s": l0_s, "l0_t": l0_t, "l0_pv": l0_pv,
                "l1_xT": xT_out("l1_xT", "l1", "l1_h", 1),
                "l1_h": h_out("l1_h", lambda g: t1, D + 2, lambda g: written(act, "l1_o", g, 1, back=1)),
                "l1_e": gat_exp("l1"),
                "l2_xT": xT_out("l2_xT", "l2", "l2_h", 1),
                "l2_h": h_out("l2_h", lambda g: t2[g.p], D + 2 * HEADS2, lambda g: wait(act, "s2_made", g, 8, back=2)),
                "l2_e": l2_e, "l2_g": l2_g, "l2_v": l2_v, "l2_md": l2_md, "l2_oT": l2_oT,
                "l3_xT": xT_out("l3_xT", "l3", "l3_m1", 1), "l3_m1": l3_m1, "l3_h": l3_h, "l3_e": gat_exp("l3"),
                "l3_elu": elu("3", e3), "l3_m2": l3_m2,
                "l3_h2": h_out("l3_h2", lambda g: t4, D + 2, lambda g: written(act, "l3_o2", g, 1, back=1)),
                "l3_r": l3_r, "l3_e2": gat_exp("l3b"), "l3_elu2": elu("4", e4),
            })

        @block.vector
        def _(dve):
            dve.wait_ge(s_adj, 16)
            adj_p = adj_i.rearrange("p c (q j) -> p c j q", j=C)
            for c in range(C):
                m = mask_add[:, c, :].rearrange("p (j q) -> p j q", j=C)
                dve.tensor_scalar(m, adj_p[:, c, :, :], 0.0, MASKED, ALU.is_equal, ALU.mult)
                last = dve.tensor_scalar(adj_m[:, c, :].rearrange("p (j q) -> p j q", j=C), adj_p[:, c, :, :], 0.0, None,
                                         ALU.is_gt)
            last.then_inc(s_pre_dve, 2)
            dve.wait_ge(s_w, 16 * N_WEIGHT_DMAS)

            tmp = v3[:, :, :].rearrange("p c n -> p (c n)")
            steps = [0]

            def fold_in(dst, wsrc, vec, shape=None):
                n = wsrc.shape[-1] if shape is None else shape[0] * shape[1]
                t = tmp[:, 0:n]
                tv = t if shape is None else t.rearrange("p (h o) -> p h o", h=shape[0])
                steps[0] += 1
                dve.tensor_tensor(t, wsrc, vec, ALU.mult).then_inc(fold_sem, 1)
                dve.wait_ge(fold_sem, steps[0])
                steps[0] += 1
                dve.tensor_reduce(dst, tv, AX_X, ALU.add).then_inc(fold_sem, 1)
                dve.wait_ge(fold_sem, steps[0])

            fold_in(w1_cat[:, 0:1], w1_cat[:, 2:2 + D], foldv[:, 0:D])
            fold_in(w1_cat[:, 1:2], w1_cat[:, 2:2 + D], foldv[:, D:2 * D])
            fold_in(w2_cat[:, D:D + HEADS2], w2_cat[:, 0:D], foldv[:, 256:384], (HEADS2, DH2))
            fold_in(w2_cat[:, D + HEADS2:D + 2 * HEADS2], w2_cat[:, 0:D], foldv[:, 384:512], (HEADS2, DH2))
            for q in range(2):
                fold_in(w3_fc[:, q, 0:1], w3_fc[:, q, 2:2 + HID], foldv[:, 512:768])
                fold_in(w3_fc[:, q, 1:2], w3_fc[:, q, 2:2 + HID], foldv[:, 768:1024])
            fold_in(w3_hand[:, 0:1], w3_hand[:, 2:2 + D], foldv[:, 1024:1152])
            fold_in(w3_hand[:, 1:2], w3_hand[:, 2:2 + D], foldv[:, 1152:1280])
            dve.memset(pre[:, 6:7], PRIOR_EPS)
            dve.tensor_scalar(pre[:, 1:2], pre[:, 0:1], 0.0, None, ALU.max)
            steps[0] += 1
            dve.tensor_scalar(pre[:, 7:8], pre[:, 0:1], -1.0, None, ALU.mult).then_inc(fold_sem, 1)
            dve.wait_ge(fold_sem, steps[0])
            dve.tensor_tensor(pre[:, 2:3], pre[:, 0:1], pre[:, 7:8], ALU.min).then_inc(s_pre_dve, 2)
            dve.wait_ge(s_setup, 1)
            steps[0] += 1
            dve.tensor_tensor(pre[:, 1:2], pre[:, 1:2], pre[:, 4:5], ALU.add).then_inc(fold_sem, 1)
            dve.wait_ge(fold_sem, steps[0])
            dve.wait_ge(s_pre_act, 5)
            dve.tensor_tensor(ln_prior[:, :], pre[:, 1:2], pre[:, 5:6], ALU.mult).then_inc(s_setup, 1)

            def l0_qk(n, bias):
                def f(g, k):
                    written(dve, "l0_" + n, g)
                    wait(dve, n + "_high", g, 1)
                    if n == "q":
                        wait(dve, "k_split", g, 1, back=1)
                    else:
                        wait(dve, "q_split", g, 1)
                    got(dve.scalar_tensor_tensor(rest[:, :], bank("l0_" + n)[:, :], bias[:, 0:1], piece[n][:, 0, :],
                                                 ALU.add, ALU.subtract), "l0_" + n)
                return f

            def l0_v(g, k):
                written(dve, "l0_v", g)
                wait(dve, "rden0_out", g, 4, back=2)
                got(dve.tensor_tensor(v0[g.p][:, :, :], bank("l0_v")[:, :].rearrange("p (c n) -> p c n", c=C),
                                      bias_v[:, :].unsqueeze(1).broadcast_to([P, C, D]), ALU.add), "l0_v")

            def l0_s(g, s):
                wait(dve, "s0_made", g, s + 1)
                mx = row_max[:, 2 * s:2 * s + 2]
                done(dve.tensor_reduce(mx, ps_s[:, :, :], AX_X, ALU.max), "max0")
                wait(dve, "max0", g, s + 1)
                done(dve.tensor_scalar(neg_max[:, 2 * s:2 * s + 2], mx, -1.0e20, -SCALE0, ALU.max, ALU.mult), "neg_max0")

            def l0_r(g, c):
                wait(dve, "exp0", g, 4 * c + 4)
                d = den0[:, 4 * c:4 * c + 4]
                done(dve.tensor_scalar(d, d, 1e-30, None, ALU.max), "den0_safe")
                wait(dve, "den0_safe", g, c + 1)
                if c:
                    written(dve, "l0_pv", g, c - 1)
                else:
                    written(dve, "l0_pv", g, C - 1, back=1)
                done(dve.reciprocal(rden0[:, :, :], d.unsqueeze(2).broadcast_to([P, HEADS0, DH0])), "rden0_made")

            def l0_pv(g, c):
                wait(dve, "rden0_out", g, c + 1)
                if c == 0:
                    written(dve, "l0_y", g, back=1)
                got(dve.tensor_tensor(o0_t[:, c * P:(c + 1) * P], bank("l0_pv", c)[:, 0:P], rden_t[:, :], ALU.mult),
                    "l0_pv", c)

            def layer_sum(n, stage, dst, base, more):
                def f(g, k):
                    written(dve, stage, g)
                    more(g)
                    got(dve.tensor_tensor(dst[g.p][:, :, :], bank(stage)[:, :].rearrange("p (c n) -> p c n", c=C),
                                          base[g.p][:, :, :], ALU.add), stage)
                return f

            def ln_stats(n, dst, summed):
                def f(g, k):
                    summed(g)
                    wait(dve, n + "_x", g, 1, back=1)
                    for c in range(C):
                        last = dve.bn_stats(stats[n][:, c, :], dst[g.p][:, c, :])
                    done(last, n + "_stats")
                    wait(dve, n + "_stats", g, 1)
                    dve.tensor_copy(waited[:, 0:1], neg_half[:, 0:1])
                    for c in range(C):
                        last = dve.bn_aggr(mv[n][:, c, :], stats[n][:, c, :])
                    done(last, n + "_mv")
                return f

            def ln_apply(n, dst):
                def f(g, k):
                    wait(dve, n + "_rstd", g, 1)
                    for c in range(C):
                        last = dve.tensor_scalar(dst[g.p][:, c, :], dst[g.p][:, c, :], mv[n][:, c, 0:1], rstd[n][:, c:c + 1],
                                                 ALU.subtract, ALU.mult)
                    done(last, n + "_x")
                return f

            def gat_small(n, stage, t):
                def f(g, k):
                    q = gat[n]
                    written(dve, stage, g, 0, 0)
                    got(dve.tensor_reduce(q["ndmax"][:, :], bank(stage, 0, 0)[:, :], AX_X, ALU.max, negate=True), stage, 0, 0)
                    drained(dve, stage, g, 0, 0)
                    wait(dve, n + "_b", g, 2, back=1)
                    done(dve.tensor_scalar(q["dd"][:, :], t[:, :, 1], q["ndmax"][:, 0:1], None, ALU.add), n + "_dd")
                    written(dve, stage, g, 0, 1)
                    wait(dve, n + "_P", g, 4, back=1)
                    got(dve.tensor_scalar(q["R"][:, :], bank(stage, 0, 1)[:, :], q["ndmax"][:, 0:1], CAP,
                                          ALU.subtract, ALU.max), stage, 0, 1)
                return f

            def gat_weights(n, reader, rk):
                def f(g, k):
                    q = gat[n]
                    wait(dve, n + "_R", g, 1)
                    wait(dve, n + "_b", g, 2)
                    written(dve, reader, g, rk, back=1)
                    for j in range(C):
                        done(dve.tensor_scalar(q["P"][:, j, :], q["R"][:, :], q["g"][:, j:j + 1], q["b"][:, j:j + 1],
                                               ALU.mult, ALU.max), n + "_P")
                return f

            def l1_o(g, k):
                q = gat["l1"]
                written(dve, "l1_o", g, k)
                ps = bank("l1_o", k)
                done(dve.reciprocal(q["rden"][:, 2 * k:2 * k + 2],
                                    ps[:, 0:2 * (D + 1)].rearrange("p (c n) -> p c n", c=2)[:, :, D]), "l1_rden")
                wait(dve, "l1_rden", g, k + 1)
                if k == 0:
                    wait(dve, "l2_x", g, 1, back=2)
                for c in range(2):
                    i = 2 * k + c
                    last = dve.scalar_tensor_tensor(x2[g.p][:, i, :], ps[:, c * (D + 1):c * (D + 1) + D], q["rden"][:, i:i + 1],
                                                    x1[g.p][:, i, :], ALU.mult, ALU.add)
                got(last, "l1_o", k)

            def l2_dm(g, k):
                written(dve, "l2_dm", g)
                got(dve.tensor_reduce(dmax8[:, :], bank("l2_dm")[0:HEADS2, :], AX_X, ALU.max), "l2_dm")
                drained(dve, "l2_dm", g)
                written(dve, "l2_db", g, back=1)
                done(dve.tensor_scalar(dmax_diag[:, :], ident[0:HEADS2, 0:HEADS2], dmax8[:, 0:1], None, ALU.mult), "dmax8_diag")

            def l2_db(g, k):
                written(dve, "l2_db", g)
                got(dve.tensor_copy(dmax_all[:, :], bank("l2_db")[:, 0:HEADS2]), "l2_db")
                drained(dve, "l2_db", g)
                d = t2[g.p][:, :, D + HEADS2:D + 2 * HEADS2]
                s = t2[g.p][:, :, D:D + HEADS2]
                m = dmax_all[:, :].unsqueeze(1).broadcast_to([P, C, HEADS2])
                wait(dve, "exp2", g, 3, back=1)
                dve.tensor_tensor(small2[:, 0, :, :], d, m, ALU.subtract)
                dve.tensor_scalar(neg_d[g.p][:, :, :], d, -1.0, None, ALU.mult)
                done(dve.tensor_tensor(small2[:, 1, :, :], s, m, ALU.add), "small2_made")
                wait(dve, "small2_made", g, 1)
                done(dve.tensor_scalar(small2[:, 1, :, :], small2[:, 1, :, :], CAP, None, ALU.max), "small2_made")

            def l2_g(g, k):
                wait(dve, "exp2", g, 3)
                wait(dve, "gl2", g, 1, back=1)
                h = t2[g.p][:, :, 0:D].rearrange("p c (h o) -> p c h o", h=HEADS2)
                G4 = G[:, :, :].rearrange("p (c h) n -> p c h n", c=C)
                for q in range(2):
                    e = bg2[:, q, :, :]
                    done(dve.tensor_tensor(G4[:, :, :, q * (DH2 + 1):q * (DH2 + 1) + DH2], h,
                                           e.unsqueeze(3).broadcast_to([P, C, HEADS2, DH2]), ALU.mult), "g2_made")
                    done(dve.tensor_copy(G4[:, :, :, q * (DH2 + 1) + DH2], e), "g2_made")

            def l2_s(g, h):
                wait(dve, "s2_made", g, h + 1)
                wait(dve, "v2_made", g, h - 1)
                for j in range(C):
                    last = dve.scalar_tensor_tensor(B1[h % 2][:, j, :], ps_b[:, :], neg_d[g.p][:, j, h:h + 1], mask_t[:, j, :],
                                                    ALU.is_ge, ALU.mult)
                done(last, "b1_made")

            def l2_c(g, k):
                wait(dve, "c2", g, 3)
                hv = MD[:, :, :].rearrange("p c (h n) -> p (c h) n", h=HEADS2)
                done(dve.reciprocal(rden2[:, :, :].rearrange("p c h -> p (c h)"), hv[:, :, DH2]), "rden2_made")
                wait(dve, "rden2_made", g, 1)
                written(dve, "l2_oT", g, back=1)
                done(dve.tensor_tensor(O2[:, :, :].rearrange("p c (h o) -> p (c h) o", h=HEADS2), hv[:, :, 0:DH2],
                                       rden2[:, :, :].rearrange("p c h -> p (c h)").unsqueeze(2)
                                       .broadcast_to([P, C * HEADS2, DH2]), ALU.mult), "o2_made")

            def l3_o(g, c):
                q = gat["l3"]
                written(dve, "l3_o", g, c)
                ps = bank("l3_o", c)
                done(dve.reciprocal(q["rden"][:, c:c + 1], ps[:, HID:HID + 1]), "l3_rden")
                wait(dve, "l3_rden", g, c + 1)
                if c == 0:
                    written(dve, "l3_zT", g, 1, back=1)
                got(dve.tensor_scalar(v3[:, c, :], ps[:, 0:HID], q["rden"][:, c:c + 1], None, ALU.mult), "l3_o", c)

            def l3_elu(g, k):
                drained(dve, "l3_o", g, C - 1)
                wait(dve, "z3_made", g, 1, back=1)
                done(dve.tensor_scalar(e3[:, :, :], v3[:, :, :], 0.0, None, ALU.min), "u3_made")
                wait(dve, "e3_made", g, 1)
                done(dve.scalar_tensor_tensor(v3[:, :, :], e3[:, :, :], -1.0, v3[:, :, :], ALU.add, ALU.max), "z3_made")

            def l3_zT(g, k):
                written(dve, "l3_zT", g, k)
                got(dve.tensor_tensor(h3_t[:, k, :], bank("l3_zT", k)[:, :], h3_t[:, k, :], ALU.add), "l3_zT", k)

            def l3_o2(g, k):
                q = gat["l3b"]
                written(dve, "l3_o2", g, k)
                ps = bank("l3_o2", k)
                done(dve.reciprocal(q["rden"][:, 2 * k:2 * k + 2],
                                    ps[:, 0:2 * (D + 1)].rearrange("p (c n) -> p c n", c=2)[:, :, D]), "l3b_rden")
                wait(dve, "l3b_rden", g, k + 1)
                if k == 0:
                    wait(dve, "stored", g, 16, back=1)
                for c in range(2):
                    i = 2 * k + c
                    last = dve.tensor_scalar(v4[:, i, :], ps[:, c * (D + 1):c * (D + 1) + D], q["rden"][:, i:i + 1], None,
                                             ALU.mult)
                got(last, "l3_o2", k)

            def l3_elu2(g, k):
                drained(dve, "l3_o2", g, 1)
                done(dve.tensor_scalar(e4[:, :, :], v4[:, :, :], 0.0, None, ALU.min), "u4_made")

            def l3_f(g, k):
                wait(dve, "e4_made", g, 1)
                drained(dve, "l3_r", g)
                done(dve.scalar_tensor_tensor(v4[:, :, :], e4[:, :, :], -1.0, v4[:, :, :], ALU.add, ALU.max), "z4")
                wait(dve, "z4", g, 1)
                done(dve.tensor_tensor(v4[:, :, :], v4[:, :, :], out2[:, :, :], ALU.add), "z4")
                wait(dve, "z4", g, 2)
                dve.scalar_tensor_tensor(x4[g.p][:, :, :], v4[:, :, :], 0.0, x3[g.p][:, :, :], ALU.max, ALU.add)\
                   .then_inc(named["l3_sum"], 1)
                ln_stats("l3", x4, lambda g: wait(dve, "l3_sum", g, 1))(g, k)

            run_bodies(dve, {
                "l0_q": l0_qk("q", bias_q), "l0_k": l0_qk("k", bias_k), "l0_v": l0_v, "l0_s": l0_s, "l0_r": l0_r, "l0_pv": l0_pv,
                "l0_y": layer_sum("l0", "l0_y", x1, x_in,
                                  lambda g: (wait(dve, "x_biased", g, 1), wait(dve, "l1_x", g, 1, back=2))),
                "l0_ln": ln_stats("l0", x1, lambda g: drained(dve, "l0_y", g)), "l0_nrm": ln_apply("l0", x1),
                "l1_sd": gat_small("l1", "l1_sd", t1), "l1_p": gat_weights("l1", "l1_o", 1), "l1_o": l1_o,
                "l1_ln": ln_stats("l1", x2, lambda g: drained(dve, "l1_o", g, 1)), "l1_nrm": ln_apply("l1", x2),
                "l2_dm": l2_dm, "l2_db": l2_db, "l2_g": l2_g, "l2_s": l2_s, "l2_c": l2_c,
                "l2_y": layer_sum("l2", "l2_y", x3, x2,
                                  lambda g: wait(dve, "l3_x", g, 1, back=2)),
                "l2_ln": ln_stats("l2", x3, lambda g: drained(dve, "l2_y", g)), "l2_nrm": ln_apply("l2", x3),
                "l3_sd": gat_small("l3", "l3_sd", t3), "l3_p": gat_weights("l3", "l3_o", 3), "l3_o": l3_o, "l3_elu": l3_elu,
                "l3_zT": l3_zT, "l3_sd2": gat_small("l3b", "l3_sd2", t4), "l3_p2": gat_weights("l3b", "l3_o2", 1),
                "l3_o2": l3_o2, "l3_elu2": l3_elu2, "l3_f": l3_f, "l3_nrm": ln_apply("l3", x4),
            })

        @block.gpsimd
        def _(pool):
            pool.memset(ident[:, :], 0.0).then_inc(s_const, 1)
            pool.memset(ones[:, :], 1.0)
            pool.memset(neg_half[:, :], -0.5)
            pool.memset(neg_one[:, :], -1.0)
            pool.memset(ln_eps[:, :], LN_EPS)
            pool.memset(t1[:, :, D + 2:D + 3], 1.0)
            pool.memset(t4[:, :, D + 2:D + 3], 1.0)
            pool.memset(t3[:, :, HID + 2:HID + 3], 1.0).then_inc(s_const, 1)
            pool.wait_ge(s_const, 2)
            pool.affine_select(out=ident[:, :], in_=ident[:, :], compare_op=ALU.not_equal, fill=1.0, base=0,
                               pattern=[[-1, P]], channel_multiplier=1).then_inc(s_const, 1)
            pool.wait_ge(s_const, 3)
            pool.tensor_copy(ident_b[:, :], ident[:, :]).then_inc(s_const, 1)
            pool.wait_ge(s_const, 4)
            pool.wait_ge(s_setup, 2)

            def l0_xT(g, k):
                wait(pool, "x_loaded", g, 16)
                written(pool, "l0_xT", g)
                done(pool.tensor_tensor(x_in[g.p][:, :, :], x_in[g.p][:, :, :],
                                        bias_o[:, :].unsqueeze(1).broadcast_to([P, C, D]), ALU.add), "x_biased")

            def l0_qk(n):
                def f(g, k):
                    drained(pool, "l0_" + n, g)
                    done(pool.tensor_tensor(piece[n][:, 1, :], rest[:, :], ones[:, 0:1].broadcast_to([P, N_NODES]), ALU.mult),
                         n + "_mid")
                    wait(pool, n + "_mid", g, 1)
                    done(pool.tensor_tensor(piece[n][:, 2, :], rest[:, :], piece[n][:, 1, :], ALU.subtract), n + "_split")
                return f

            def ln_rstd(n):
                def f(g, k):
                    wait(pool, n + "_mv", g, 1)
                    wait(pool, n + "_x", g, 1, back=1)
                    done(pool.tensor_tensor(rstd[n][:, :], mv[n][:, :, 1], ln_eps[:, :], ALU.add), n + "_var")
                    wait(pool, n + "_var", g, 1)
                    done(pool.tensor_tensor(rstd[n][:, :], rstd[n][:, :], neg_half[:, :], ALU.pow), n + "_rstd")
                return f

            def mask_weights(n):
                def f(g, k):
                    for j in range(C):
                        wait(pool, n + "_P", g, j + 1)
                        t = gat[n]["P"][:, j, :]
                        done(pool.tensor_tensor(t, t, mask_t[:, j, :], ALU.mult), n + "_Pm")
                return f

            def l2_g(g, k):
                wait(pool, "gh2", g, 1)
                done(pool.tensor_tensor(G[:, :, :], G[:, :, :], GS[g.p][:, :, 0, :], ALU.subtract), "gr2")
                wait(pool, "gr2", g, 1)
                done(pool.tensor_tensor(GS[g.p][:, :, 1, :], G[:, :, :],
                                        ones[:, 0:1].unsqueeze(2).broadcast_to([P, C * HEADS2, W2C]), ALU.mult), "gm2")
                wait(pool, "gm2", g, 1)
                done(pool.tensor_tensor(GS[g.p][:, :, 2, :], G[:, :, :], GS[g.p][:, :, 1, :], ALU.subtract), "gl2")

            def l2_v(g, h):
                wait(pool, "v2_out", g, h + 1)
                if h == 0:
                    wait(pool, "c2", g, 3, back=1)
                e = EV[h % 2]
                done(pool.tensor_tensor(U[:, h, :, :], e[:, :, 0, :], e[:, :, 1, :], ALU.add), "u2_made")
                wait(pool, "u2_made", g, 2 * h + 1)
                done(pool.tensor_tensor(U[:, h, :, :], U[:, h, :, :], e[:, :, 2, :], ALU.add), "u2_made")

            def l2_c(g, k):
                wait(pool, "u2_made", g, 16)
                drained(pool, "l2_md", g, 0)
                drained(pool, "l2_md", g, 1)
                m = MD[:, :, :].rearrange("p c (h n) -> p h c n", h=HEADS2)
                for c in range(C):
                    mc = MD[:, c, :].rearrange("p (h n) -> p h n", h=HEADS2)
                    last = pool.tensor_tensor(mc, mc, U[:, :, c, DH2 + 1:W2C], ALU.subtract)
                done(last, "c2")
                wait(pool, "c2", g, 1)
                mm = MD[:, :, :].rearrange("p c (h n) -> p (c h) n", h=HEADS2)
                done(pool.tensor_tensor(mm, mm, R2[g.p][:, :, :].rearrange("p c h -> p (c h)").unsqueeze(2)
                                        .broadcast_to([P, C * HEADS2, DH2 + 1]), ALU.mult), "c2")
                wait(pool, "c2", g, 2)
                for c in range(C):
                    mc = MD[:, c, :].rearrange("p (h n) -> p h n", h=HEADS2)
                    last = pool.tensor_tensor(mc, mc, U[:, :, c, 0:DH2 + 1], ALU.add)
                done(last, "c2")

            run_bodies(pool, {
                "l0_xT": l0_xT, "l0_q": l0_qk("q"), "l0_k": l0_qk("k"),
                "l0_ln": ln_rstd("l0"), "l1_ln": ln_rstd("l1"), "l2_ln": ln_rstd("l2"), "l3_f": ln_rstd("l3"),
                "l1_p": mask_weights("l1"), "l3_p2": mask_weights("l3b"), "l2_g": l2_g, "l2_v": l2_v, "l2_c": l2_c,
            })


_WEIGHTS = ['L0_gnn_wq', 'L0_gnn_bq', 'L0_gnn_wk', 'L0_gnn_bk', 'L0_gnn_wv', 'L0_gnn_bv', 'L0_gnn_wo', 'L0_gnn_bo',
            'L1_gnn_W', 'L1_gnn_a', 'L2_gnn_W', 'L2_gnn_a_src', 'L2_gnn_a_dst', 'L2_gnn_beta_tilde', 'L2_gnn_W_out',
            'L3_gnn_mlp1_w', 'L3_gnn_mlp1_b', 'L3_gnn_mlp2_w', 'L3_gnn_mlp2_b', 'L3_gnn_W_fc', 'L3_gnn_a_fc',
            'L3_gnn_W_hand', 'L3_gnn_a_hand']


def kernel(**inputs):
    import numpy as _np
    import concourse.bacc as _bacc
    from concourse import mybir as _mybir
    from concourse.bass_utils import run_bass_kernel_spmd as _run

    nc = _bacc.Bacc("TRN2", target_bir_lowering=False, num_devices=1)
    arrays, aps = {}, {}
    for name in ['x', 'adj'] + _WEIGHTS:
        a = _np.atleast_1d(_np.asarray(inputs[name]))
        a = _np.ascontiguousarray(a)
        arrays[f"in_{name}"] = a
        aps[name] = nc.dram_tensor(f"in_{name}", a.shape, _mybir.dt.from_np(a.dtype), kind="ExternalInput").ap()
    out = nc.dram_tensor("out", (N_GRAPHS, N_NODES, D), F32, kind="ExternalOutput").ap()
    build_program(nc, aps['x'], aps['adj'], {n: aps[n] for n in _WEIGHTS}, out)
    r = _run(nc, [arrays], core_ids=[0])
    return _np.asarray(r.results[0]["out"])
```

```python
from contextlib import ExitStack

import concourse.bass as bass
from concourse import mybir

P = 128
N_GRAPHS, N_NODES, D = 16, 512, 128
C = N_NODES // P
HEADS0, DH0 = 4, 32
HEADS2, DH2 = 8, 16
HID = 256
F32, BF16, I32 = mybir.dt.float32, mybir.dt.bfloat16, mybir.dt.int32
ALU = mybir.AluOpType
ACT = mybir.ActivationFunctionType
AX_X = mybir.AxisListType.X
SCALE0 = float(DH0) ** -0.5
MASKED = -1.0e30
LN_EPS = 1e-5
PRIOR_EPS = 1e-6
CAP = -75.0
W2C = 2 * (DH2 + 1)

SCHEDULE = {
    "sp": [
        ("x_load", 0, 0), ("l0_q", 0, 0), ("l0_k", 0, 0), ("store", 0, 4),
    ],
    "pe": [
        ("l3_o", 3, 4), ("l0_pv", 0, 1), ("l2_s", 7, 3), ("l2_v", 6, 3), ("l0_s", 6, 1), ("l0_s", 7, 1),
        ("l1_o", 0, 2), ("l1_o", 1, 2), ("l0_t", 4, 1), ("l2_v", 7, 3), ("l3_zT", 0, 4), ("l0_t", 5, 1),
        ("l0_s", 8, 1), ("l3_zT", 1, 4), ("l0_s", 9, 1), ("l0_t", 6, 1), ("l0_t", 7, 1), ("l3_m2", 0, 4),
        ("l0_pv", 1, 1), ("l0_s", 10, 1), ("l0_s", 11, 1), ("l3_h2", 0, 4), ("l3_h2", 1, 4), ("l0_t", 8, 1),
        ("l2_xT", 0, 2), ("l3_sd2", 0, 4), ("l2_h", 0, 2), ("l2_oT", 0, 3), ("l0_s", 12, 1), ("l3_sd2", 1, 4),
        ("l2_y", 0, 3), ("l2_h", 1, 2), ("l0_s", 13, 1), ("l0_t", 9, 1), ("l2_dm", 0, 2), ("l0_xT", 0, 0),
        ("l0_t", 10, 1), ("l0_t", 11, 1), ("l0_q", 0, 0), ("l2_db", 0, 2), ("l2_s", 0, 2), ("l0_s", 14, 1),
        ("l0_pv", 2, 1), ("l0_s", 15, 1), ("l0_k", 0, 0), ("l0_t", 12, 1), ("l0_t", 13, 1), ("l3_xT", 0, 3),
        ("l2_s", 1, 2), ("l0_v", 0, 0), ("l3_o2", 0, 4), ("l3_m1", 0, 3), ("l0_t", 14, 1), ("l3_o2", 1, 4),
        ("l3_m1", 1, 3), ("l0_t", 15, 1), ("l2_s", 2, 2), ("l0_pv", 3, 1), ("l3_h", 0, 3), ("l0_y", 0, 1),
        ("l2_v", 0, 2), ("l3_h", 1, 3), ("l3_h", 2, 3), ("l3_h", 3, 3), ("l3_r", 0, 4), ("l2_v", 1, 2),
        ("l3_sd", 0, 3), ("l3_sd", 1, 3), ("l0_s", 0, 0), ("l2_s", 3, 2), ("l0_s", 1, 0), ("l2_md", 0, 2),
        ("l2_md", 1, 2), ("l2_v", 2, 2), ("l2_s", 4, 2), ("l1_xT", 0, 1), ("l2_v", 3, 2), ("l0_s", 2, 0),
        ("l1_h", 0, 1), ("l1_h", 1, 1), ("l0_s", 3, 0), ("l3_o", 0, 3), ("l1_sd", 0, 1), ("l0_t", 0, 0),
        ("l2_s", 5, 2), ("l1_sd", 1, 1), ("l0_s", 4, 0), ("l2_v", 4, 2), ("l3_o", 1, 3), ("l0_s", 5, 0),
        ("l0_t", 1, 0), ("l3_o", 2, 3), ("l0_t", 2, 0), ("l0_t", 3, 0), ("l2_s", 6, 2), ("l2_v", 5, 2),
    ],
    "act": [
        ("l0_t", 4, 1), ("l0_exp", 7, 1), ("l0_t", 5, 1), ("l0_t", 6, 1), ("l0_t", 7, 1), ("l0_exp", 8, 1),
        ("l3_m2", 0, 4), ("l0_exp", 9, 1), ("l0_rden", 1, 1), ("l1_norm", 0, 2), ("l3_h2", 0, 4), ("l3_h2", 1, 4),
        ("l2_xT", 0, 2), ("l0_exp", 10, 1), ("l2_h", 0, 2), ("l3_e2", 0, 4), ("l2_oT", 0, 3), ("l0_exp", 11, 1),
        ("l3_R2", 0, 4), ("l2_h", 1, 2), ("l0_t", 8, 1), ("l0_t", 9, 1), ("l0_xT", 0, 0), ("l0_t", 10, 1),
        ("l0_q", 0, 0), ("l0_t", 11, 1), ("l2_norm", 0, 3), ("l0_exp", 12, 1), ("l2_e", 0, 2), ("l0_rden", 2, 1),
        ("l0_exp", 13, 1), ("l0_k", 0, 0), ("l3_xT", 0, 3), ("l0_t", 12, 1), ("l0_t", 13, 1), ("l0_exp", 14, 1),
        ("l2_high", 0, 2), ("l3_v2", 0, 4), ("l3_m1", 0, 3), ("l0_exp", 15, 1), ("l0_t", 14, 1), ("l3_v2", 1, 4),
        ("l3_m1", 1, 3), ("l0_t", 15, 1), ("l3_elu2", 0, 4), ("l0_rden", 3, 1), ("l3_h", 0, 3), ("l2_v", 0, 2),
        ("l3_h", 1, 3), ("l3_h", 2, 3), ("l3_h", 3, 3), ("l3_e", 0, 3), ("l2_v", 1, 2), ("l3_R", 0, 3),
        ("l2_md", 0, 2), ("l0_norm", 0, 1), ("l2_v", 2, 2), ("l2_md", 1, 2), ("l1_xT", 0, 1), ("l1_h", 0, 1),
        ("l1_h", 1, 1), ("l0_exp", 0, 0), ("l2_v", 3, 2), ("l0_exp", 1, 0), ("l3_v", 0, 3), ("l0_t", 0, 0),
        ("l0_exp", 2, 0), ("l1_R", 0, 1), ("l0_exp", 3, 0), ("l2_v", 4, 2), ("l1_e", 0, 1), ("l0_t", 1, 0),
        ("l0_t", 2, 0), ("l3_v", 1, 3), ("l0_t", 3, 0), ("l3_v", 2, 3), ("l3_norm", 0, 4), ("l3_v", 3, 3),
        ("l2_v", 5, 2), ("l0_rden", 0, 0), ("l3_elu", 0, 3), ("l2_v", 6, 2), ("l0_exp", 4, 0), ("l0_exp", 5, 0),
        ("l1_v", 0, 1), ("l1_v", 1, 1), ("l0_exp", 6, 0), ("l2_v", 7, 2),
    ],
    "dve": [
        ("l0_den", 0, 1), ("l1_p", 2, 2), ("l3_rcp", 2, 4), ("l0_rcp", 0, 1), ("l2_signs", 6, 3), ("l3_rcp", 3, 4),
        ("l1_p", 3, 2), ("l0_max", 2, 1), ("l0_o", 0, 1), ("l0_neg", 2, 1), ("l2_signs", 7, 3), ("l0_max", 3, 1),
        ("l1_rcp", 0, 2), ("l1_rcp", 1, 2), ("l0_neg", 3, 1), ("l3_z", 0, 4), ("l1_stats", 0, 2), ("l3_zT", 0, 4),
        ("l3_zT", 1, 4), ("l0_max", 4, 1), ("l0_den", 1, 1), ("l0_neg", 4, 1), ("l0_rcp", 1, 1), ("l1_aggr", 0, 2),
        ("l0_o", 1, 1), ("l0_max", 5, 1), ("l2_rcp", 0, 3), ("l0_neg", 5, 1), ("l3_dmax2", 0, 4), ("l3_dd2", 0, 4),
        ("l3_s2", 0, 4), ("l2_y", 0, 3), ("l3_p2", 0, 4), ("l2_stats", 0, 3), ("l2_dm", 0, 2), ("l2_aggr", 0, 3),
        ("l2_diag", 0, 2), ("l0_max", 6, 1), ("l3_p2", 1, 4), ("l3_p2", 2, 4), ("l0_den", 2, 1), ("l0_neg", 6, 1),
        ("l0_q", 0, 0), ("l0_rcp", 2, 1), ("l2_db", 0, 2), ("l3_p2", 3, 4), ("l2_small", 0, 2), ("l2_cap", 0, 2),
        ("l2_signs", 0, 2), ("l0_o", 2, 1), ("l0_k", 0, 0), ("l0_max", 7, 1), ("l0_neg", 7, 1), ("l0_v", 0, 0),
        ("l3_rcp2", 0, 4), ("l2_signs", 1, 2), ("l3_rcp2", 1, 4), ("l0_den", 3, 1), ("l0_rcp", 3, 1), ("l0_o", 3, 1),
        ("l3_z2", 0, 4), ("l0_y", 0, 1), ("l2_signs", 2, 2), ("l0_stats", 0, 1), ("l3_sum", 0, 4), ("l3_dmax", 0, 3),
        ("l0_aggr", 0, 1), ("l3_dd", 0, 3), ("l3_s", 0, 3), ("l2_signs", 3, 2), ("l3_p", 0, 3), ("l0_max", 0, 0),
        ("l3_p", 1, 3), ("l3_p", 2, 3), ("l0_neg", 0, 0), ("l3_p", 3, 3), ("l2_signs", 4, 2), ("l3_y", 0, 4),
        ("l3_rcp", 0, 3), ("l0_max", 1, 0), ("l1_dmax", 0, 1), ("l3_stats", 0, 4), ("l0_neg", 1, 0), ("l3_aggr", 0, 4),
        ("l1_dd", 0, 1), ("l1_s", 0, 1), ("l2_signs", 5, 2), ("l1_p", 0, 1), ("l1_p", 1, 1), ("l3_rcp", 1, 3),
    ],
    "pool": [
        ("l1_mask", 0, 2), ("l1_mask", 1, 2), ("l2_u", 4, 3), ("l1_mask", 2, 2), ("l2_w", 3, 3), ("l1_mask", 3, 2),
        ("l2_w", 4, 3), ("l2_u", 5, 3), ("l2_w", 5, 3), ("l2_u", 6, 3), ("l2_w", 6, 3), ("l1_y", 0, 2), ("l2_u", 7, 3),
        ("l2_w", 7, 3), ("l2_c", 0, 3), ("l2_c", 1, 3), ("l1_var", 0, 2), ("l1_pow", 0, 2), ("l1_shift", 0, 2),
        ("l2_c", 2, 3), ("l2_o", 0, 3), ("l3_mask2", 0, 4), ("l2_var", 0, 3), ("l2_pow", 0, 3), ("l2_shift", 0, 3),
        ("l3_mask2", 1, 4), ("l3_mask2", 2, 4), ("l0_q", 0, 0), ("l0_q", 1, 0), ("l3_mask2", 3, 4), ("l2_g", 0, 2),
        ("l2_g", 1, 2), ("l0_k", 0, 0), ("l0_k", 1, 0), ("l2_split", 0, 2), ("l2_split", 1, 2), ("l2_split", 2, 2),
        ("l0_var", 0, 1), ("l0_pow", 0, 1), ("l2_u", 0, 2), ("l0_shift", 0, 1), ("l2_u", 1, 2), ("l2_w", 0, 2),
        ("l2_w", 1, 2), ("l0_bias", 0, 0), ("l3_var", 0, 4), ("l2_u", 2, 2), ("l2_w", 2, 2), ("l3_pow", 0, 4),
        ("l2_u", 3, 2), ("l3_shift", 0, 4),
    ],
}
LAST_LAG = max(lag for order in SCHEDULE.values() for _, _, lag in order)
BODIES = N_GRAPHS + LAST_LAG
LOOP_FROM = LAST_LAG + 1 + (LAST_LAG + 1) % 2
LOOP_TO = N_GRAPHS - (N_GRAPHS - LOOP_FROM) % 2
PE_LAG = {(name, k): lag for name, k, lag in SCHEDULE["pe"]}

RING_USES = {"l0_xT": 1, "l0_q": 1, "l0_k": 1, "l0_v": 1, "l0_pv": 1, "l0_y": 1,
             "l1_xT": 1, "l1_h": 1, "l1_sd": 1, "l1_o": 1,
             "l2_xT": 1, "l2_h": 1, "l2_dm": 1, "l2_db": 1, "l2_md": 1, "l2_oT": 1, "l2_y": 1,
             "l3_xT": 1, "l3_m1": 1, "l3_h": 1, "l3_sd": 1, "l3_o": 1, "l3_zT": 1, "l3_m2": 1,
             "l3_h2": 1, "l3_r": 1, "l3_sd2": 1, "l3_o2": 1}
RING = 2


class Graph:

    def __init__(self, i, parity, least):
        self.i, self.p, self.least = i, parity % 2, least

    def has(self, back):
        return not isinstance(self.i, int) or self.i >= back

    def back(self, n):
        return Graph(self.i - n, self.p + n, self.least - n)


def ring_counts():
    uses = [e for e in SCHEDULE["pe"] if e[0] in RING_USES]
    bank = {(name, k): at % RING for at, (name, k, _) in enumerate(uses)}
    used, before = [0] * RING, []
    for t in range(BODIES):
        now = {}
        for name, k, lag in uses:
            now[name, k] = used[bank[name, k]]
            used[bank[name, k]] += 0 <= t - lag < N_GRAPHS
        before.append(now)
    return bank, before


def build_program(nc, x, adj, w, out):
    bank_of, uses_before = ring_counts()

    with ExitStack() as ctx:
        def sb(name, shape, dt=F32):
            return ctx.enter_context(nc.sbuf_tensor(name, shape, dt))

        def psum(name, shape):
            return ctx.enter_context(nc.psum_tensor(name, shape, F32))

        per_graph = {}

        def sem(name, n=0):
            s = ctx.enter_context(nc.semaphore(name))
            per_graph[name] = n
            signal[name] = s
            return s

        signal = {}

        ident = sb("ident", [P, P])
        ones = sb("ones", [P, P])
        neg_half = sb("neg_half", [P, C])
        mask_add = sb("mask_add", [P, C, N_NODES], BF16)
        mask_t = sb("mask_t", [P, C, N_NODES], BF16)
        wT = {n: sb(n + "T", [P, D]) for n in ("wq", "wk", "wv", "wo", "w_out")}
        bias_q, bias_k = sb("bias_q", [P, 1]), sb("bias_k", [P, 1])
        bias_v, bias_o = sb("bias_v", [P, D]), sb("bias_o", [P, D])
        w1_cat = sb("w1_cat", [P, 2 + D])
        w2_cat = sb("w2_cat", [P, D + 2 * HEADS2])
        w3a = sb("w3a", [P, HID])
        b3a = sb("b3a", [P, 2])
        w3_fc = sb("w3_fc", [P, 2, 2 + HID])
        w3b = sb("w3b", [P, 2, D])
        b3b = sb("b3b", [P, 1])
        w3_hand = sb("w3_hand", [P, 2 + D])
        ln_prior = sb("ln_prior", [P, 1])
        pre = sb("pre", [P, 8])
        neg_one = sb("neg_one", [P, C])
        waited = sb("waited", [P, 12])
        ln_eps = sb("ln_eps", [P, C])

        x_in = [sb(f"x_in{q}", [P, C, D]) for q in range(2)]
        x1 = [sb(f"x1_{q}", [P, C, D]) for q in range(2)]
        x2 = [sb(f"x2_{q}", [P, C, D]) for q in range(2)]
        x3 = [sb(f"x3_{q}", [P, C, D]) for q in range(2)]
        xT = {n: sb("xT" + n, [P, N_NODES]) for n in ("l0", "l1", "l2", "l3")}
        piece = {n: sb("piece_" + n, [P, 3, N_NODES], BF16) for n in "qk"}
        rest = sb("rest", [P, N_NODES])
        stack = {n: [[sb(f"stack_{n}{g}_{q}", [P, HEADS0, N_NODES], BF16) for g in range(2)] for q in range(2)]
                 for n in "qk"}
        v0 = [sb(f"v0_{q}", [P, C, D]) for q in range(2)]
        row_max = sb("row_max", [P, 16])
        neg_max = sb("neg_max", [P, 16])
        probs = [sb(f"probs{q}", [P, 2, N_NODES]) for q in range(2)]
        den0 = sb("den0", [P, 16])
        rden0 = sb("rden0", [P, 16])
        probs_t = sb("probs_t", [P, HEADS0, C, P])
        rden_t = sb("rden_t", [P, P])
        o0_t = sb("o0_t", [P, N_NODES])
        stats = {n: sb("stats_" + n, [P, C, 6]) for n in ("l0", "l1", "l2", "l3")}
        mv = {n: sb("mv_" + n, [P, C, 2]) for n in ("l0", "l1", "l2", "l3")}
        rstd = {n: sb("rstd_" + n, [P, C]) for n in ("l0", "l1", "l2", "l3")}
        shift = {n: sb("shift_" + n, [P, C]) for n in ("l0", "l1", "l2", "l3")}
        t1 = sb("t1", [P, C, D + 4])
        t3 = sb("t3", [P, C, HID + 4])
        t4 = sb("t4", [P, C, D + 4])
        gat = {}
        for n in ("l1", "l3", "l3b"):
            gat[n] = dict(ndmax=sb(n + "_ndmax", [P, 1]), dd=sb(n + "_dd", [P, C]), b=sb(n + "_b", [P, C]),
                          g=sb(n + "_g", [P, C]), R=sb(n + "_R", [P, N_NODES]),
                          P=sb(n + "_P", [P, C, N_NODES]), rden=sb(n + "_rden", [P, C]))
        t2 = [sb(f"t2_{q}", [P, C, D + 2 * HEADS2]) for q in range(2)]
        dmax8 = sb("dmax8", [HEADS2, 1])
        dmax_diag = sb("dmax_diag", [HEADS2, HEADS2])
        dmax_all = sb("dmax_all", [P, HEADS2])
        small2 = sb("small2", [P, 2, C, HEADS2])
        neg_d = [sb(f"neg_d{q}", [P, C, HEADS2]) for q in range(2)]
        R2 = [sb(f"R2_{q}", [P, C, HEADS2]) for q in range(2)]
        bg2 = sb("bg2", [P, 2, C, HEADS2])
        G = sb("G", [P, C * HEADS2, W2C])
        GS = [sb(f"GS{q}", [P, C * HEADS2, 3, W2C], BF16) for q in range(2)]
        B1 = [sb(f"B1_{q}", [P, C, N_NODES], BF16) for q in range(2)]
        EV = [sb(f"EV{q}", [P, C, 3, W2C]) for q in range(2)]
        U = sb("U", [P, HEADS2, C, W2C])
        MD = sb("MD", [P, C, HEADS2 * (DH2 + 1)])
        rden2 = sb("rden2", [P, C, HEADS2])
        O2 = sb("O2", [P, C, D])
        O2_t = sb("O2_t", [P, N_NODES])
        h3_t = sb("h3_t", [P, 2, N_NODES])
        v3 = sb("v3", [P, C, HID])
        e3 = sb("e3", [P, C, HID])
        out2_t = sb("out2_t", [P, N_NODES])
        v4 = sb("v4", [P, C, D])
        e4 = sb("e4", [P, C, D])
        x4 = [v4, v4]

        ps_s = psum("ps_s", [P, 2, N_NODES])
        ps_t = psum("ps_t", [P, 2, N_NODES])
        ps_b = psum("ps_b", [P, N_NODES])
        ps_v = psum("ps_v", [P, N_NODES])
        ring = [psum(f"ring{k}", [P, N_NODES]) for k in range(RING)]

        s_w = sem("weights_loaded")
        s_adj = sem("adj_loaded")
        s_const = sem("consts_made")
        s_pre_pe = sem("setup_pe")
        s_pre_dve = sem("setup_dve")
        s_pre_act = sem("setup_act")
        s_setup = sem("setup_done")
        fold_sem = sem("folded")
        ring_written = [sem(f"ring_written{k}") for k in range(RING)]
        ring_read = [sem(f"ring_read{k}") for k in range(RING)]
        for name, n in [("x_loaded", 16), ("x_biased", 1), ("q_high", 1), ("k_high", 1), ("q_mid", 1), ("k_mid", 1),
                        ("q_split", 1), ("k_split", 1), ("q_spilled", 16), ("k_spilled", 16),
                        ("q_stacked", 128), ("k_stacked", 128),
                        ("s0_made", 16), ("max0", 16), ("neg_max0", 8), ("exp0", 16), ("t0_made", 16), ("t0_out", 16),
                        ("den0_safe", 4), ("rden0_made", 4), ("rden0_out", 4),
                        ("b1_made", 8),
                        ("s2_made", 8), ("v2_made", 8), ("v2_out", 8), ("u2_first", 8), ("u2_made", 8),
                        ("dmax8_diag", 1), ("small2_made", 2), ("exp2", 3), ("g2_made", 2), ("gh2", 1),
                        ("gr2", 1), ("gm2", 1), ("gl2", 1), ("c2", 3), ("rden2_made", 1), ("o2_made", 1),
                        ("u3_made", 1), ("e3_first", 1), ("e3_made", 1), ("z3_made", 1),
                        ("u4_made", 1), ("e4_first", 1), ("e4_made", 1), ("z4", 1), ("x4_made", 1), ("x2_made", 1), ("stored", 16)]:
            sem(name, n)
        for n in ("l0", "l1", "l2", "l3"):
            sem(n + "_stats", 1)
            sem(n + "_mv", 1)
            sem(n + "_var", 2)
            sem(n + "_rstd", 1)
            sem(n + "_shift", 1)
            sem(n + "_x", 1)
        for n in ("l1", "l3", "l3b"):
            sem(n + "_dd", 1)
            sem(n + "_b", 2)
            sem(n + "_R", 1)
            sem(n + "_P", 4)
            sem(n + "_Pm", 4)
            sem(n + "_rden", 4 if n == "l3" else 2)

        def count(name, g, k, back=0):
            v = per_graph[name] * (g.i - back) + k
            assert isinstance(v, int) or per_graph[name] * (g.least - back) + k >= 1, (name, back, k)
            return v

        def wait_if_any(eng, name, g, k, back=0):
            if g.has(back):
                v = count(name, g, k, back)
                if not isinstance(v, int) or v > 0:
                    eng.wait_ge(signal[name], v)

        def uses(stage, g, k):
            t = g.i + PE_LAG[stage, k]
            if isinstance(t, int):
                return uses_before[t][stage, k]
            least = g.least + PE_LAG[stage, k]
            assert LAST_LAG <= least and least + LOOP_TO - 2 - LOOP_FROM <= N_GRAPHS, (stage, k)
            step = uses_before[LOOP_FROM + 1][stage, k] - uses_before[LOOP_FROM][stage, k]
            return (t - LOOP_FROM) * step + uses_before[LOOP_FROM][stage, k]

        def ring_wait(eng, sems, g, tickets, free=None):
            last = {}
            for stage, k, back in tickets:
                if g.has(back):
                    h = g.back(back)
                    rank = uses(stage, Graph(h.least, h.p, h.least), k) + 1
                    last[bank_of[stage, k]] = max(last.get(bank_of[stage, k], (0, 0)), (rank, uses(stage, h, k) + 1),
                                                  key=lambda v: v[0])
            if free is not None:
                n = uses(free[0], g, free[1])
                if not isinstance(n, int) or n > 0:
                    rank = uses(free[0], Graph(g.least, g.p, g.least), free[1])
                    last[bank_of[free]] = max(last.get(bank_of[free], (0, 0)), (rank, n), key=lambda v: v[0])
            for b, (_, n) in last.items():
                eng.wait_ge(sems[b], n)

        def written(eng, g, *tickets):
            ring_wait(eng, ring_written, g, tickets)

        def drained(eng, g, *tickets):
            ring_wait(eng, ring_read, g, tickets)

        def free_bank(g, stage, k=0, *tickets):
            ring_wait(nc.tensor, ring_read, g, tickets, (stage, k))
            return ring[bank_of[stage, k]]

        def bank(stage, k=0):
            return ring[bank_of[stage, k]]

        def run_bodies(eng, order, stages):
            def body(t, parity, known):
                for name, k, lag in order:
                    if known is None or 0 <= known - lag < N_GRAPHS:
                        stages[name](Graph(t - lag, parity - lag, LOOP_FROM + parity % 2 - lag if known is None else known - lag), k)
            for t in range(LOOP_FROM):
                body(t, t, t)
            with eng.Fori(LOOP_FROM, LOOP_TO - 1, 2) as t:
                body(t, 0, None)
                body(t + 1, 1, None)
            for t in range(LOOP_TO, BODIES):
                body(t, t, t)

        spill = {n: nc.dram_tensor("spill_" + n, [P, 3, N_NODES], BF16, kind="Internal").ap() for n in "qk"}
        x_v = x.rearrange("b (p c) d -> b p c d", c=C)
        out_v = out.rearrange("b (p c) d -> b p c d", c=C)
        adj_i = gat["l1"]["P"][:, :, :].bitcast(I32)
        adj_m = gat["l3"]["P"]
        raw = gat["l3b"]["P"]
        RAW = {"wq": 0, "wk": 1, "wv": 2, "wo": 3, "w_out": 4}
        fold = probs_t
        foldv = fold[:, :, :, :].rearrange("p a b c -> p (a b c)")

        block = ctx.enter_context(nc.Block())

        N_WEIGHT_DMAS = 24


        @block.sync
        def _(sp):
            sp.dma_start(adj_i, adj.rearrange("(p c) n -> p c n", c=C)).then_inc(s_adj, 16)
            rawf = raw[:, :, :].rearrange("p a b -> p (a b)")

            def load(dst, src):
                sp.dma_start(dst, src).then_inc(s_w, 16)

            def everywhere(vec, n):
                return vec.rearrange("(o n) -> o n", o=1).broadcast_to([P, n])

            for n, key in (("wq", "L0_gnn_wq"), ("wk", "L0_gnn_wk"), ("wv", "L0_gnn_wv"), ("wo", "L0_gnn_wo"),
                           ("w_out", "L2_gnn_W_out")):
                load(rawf[:, RAW[n] * D:(RAW[n] + 1) * D], w[key])
            load(bias_q[:, :], w["L0_gnn_bq"].rearrange("(p o) -> p o", o=1))
            load(bias_k[:, :], w["L0_gnn_bk"].rearrange("(p o) -> p o", o=1))
            load(bias_v[:, :], everywhere(w["L0_gnn_bv"], D))
            load(bias_o[:, :], everywhere(w["L0_gnn_bo"], D))
            load(w1_cat[:, 2:2 + D], w["L1_gnn_W"])
            load(w2_cat[:, 0:D].rearrange("p (h o) -> p h o", h=HEADS2), w["L2_gnn_W"].rearrange("h d o -> d h o"))
            load(w3a[:, :], w["L3_gnn_mlp1_w"])
            for q in range(2):
                load(b3a[:, q:q + 1], w["L3_gnn_mlp1_b"].rearrange("(k p o) -> k p o", p=P, o=1)[q])
            load(w3_fc[:, :, 2:2 + HID], w["L3_gnn_W_fc"].rearrange("(k p) n -> p k n", p=P))
            load(w3b[:, :, :], w["L3_gnn_mlp2_w"].rearrange("(k p) n -> p k n", p=P))
            load(b3b[:, :], w["L3_gnn_mlp2_b"].rearrange("(p o) -> p o", o=1))
            load(w3_hand[:, 2:2 + D], w["L3_gnn_W_hand"])
            load(foldv[:, 0:256], everywhere(w["L1_gnn_a"].rearrange("a o -> (a o)"), 256))
            load(foldv[:, 256:384], everywhere(w["L2_gnn_a_src"].rearrange("a o -> (a o)"), 128))
            load(foldv[:, 384:512], everywhere(w["L2_gnn_a_dst"].rearrange("a o -> (a o)"), 128))
            load(foldv[:, 512:1024], everywhere(w["L3_gnn_a_fc"].rearrange("a o -> (a o)"), 512))
            load(foldv[:, 1024:1280], everywhere(w["L3_gnn_a_hand"].rearrange("a o -> (a o)"), 256))
            load(pre[:, 0:1], w["L2_gnn_beta_tilde"].rearrange("(o n) -> o n", o=1).broadcast_to([P, 1]))

            def x_load(g, k):
                wait_if_any(sp, "l0_stats", g, 1, back=2)
                sp.dma_start(x_in[g.p][:, :, :], x_v[g.i]).then_inc(signal["x_loaded"], 16)

            def split(n, g):
                sp.wait_ge(signal[n + "_split"], count(n + "_split", g, 1))
                wait_if_any(sp, n + "_stacked", g, 128, back=1)
                sp.dma_start(spill[n], piece[n][:, :, :]).then_inc(signal[n + "_spilled"], 16)
                wait_if_any(sp, "s0_made", g, 16, back=2)
                sp.wait_ge(signal[n + "_spilled"], count(n + "_spilled", g, 16))
                parts = {"q": ((0, 0, 1, 1), (0, 2, 1, 2)), "k": ((0, 1, 0, 1), (2, 0, 2, 1))}[n]
                for q in range(2):
                    for blk in range(4):
                        sp.dma_start(stack[n][q][g.p][DH0 * blk:DH0 * (blk + 1), :, :],
                                     spill[n].rearrange("(h r) s n -> s r h n", h=HEADS0)[parts[q][blk]])\
                          .then_inc(signal[n + "_stacked"], 16)

            def store(g, k):
                sp.wait_ge(signal["l3_x"], count("l3_x", g, 1))
                sp.dma_start(out_v[g.i], x4[g.p][:, :, :]).then_inc(signal["stored"], 16)

            run_bodies(sp, SCHEDULE["sp"], {"x_load": x_load, "l0_q": lambda g, k: split("q", g),
                                            "l0_k": lambda g, k: split("k", g), "store": store})
            sp.wait_ge(signal["stored"], 16 * N_GRAPHS)

        @block.tensor
        def _(pe):
            pe.wait_ge(s_const, 3)
            pe.wait_ge(s_w, 16 * N_WEIGHT_DMAS)
            rawf = raw[:, :, :].rearrange("p a b -> p (a b)")
            for n in ("wq", "wk", "wv", "wo"):
                last = pe.transpose(ring[0][:, RAW[n] * D:(RAW[n] + 1) * D], rawf[:, RAW[n] * D:(RAW[n] + 1) * D], ident[:, :])
            last = pe.transpose(ring[1][:, 0:D], rawf[:, 4 * D:5 * D], ident[:, :])
            last.then_inc(s_pre_pe, 1)
            pe.wait_ge(s_pre_dve, 2)
            for j in range(C):
                pe.wait_ge(s_pre_act, j + 1)
                for c in range(C):
                    last = pe.transpose(ring[0][:, c * P:(c + 1) * P], adj_m[:, c, j * P:(j + 1) * P], ident[:, :])
                last.then_inc(s_pre_pe, 1)
            pe.wait_ge(s_setup, 2)

            def to_T(stage, src, ready):
                def f(g, k):
                    ready(g)
                    ps = free_bank(g, stage)
                    for c in range(C):
                        last = pe.transpose(ps[:, c * P:(c + 1) * P], src(g)[:, c, :], ident[:, :])
                    last.then_inc(ring_written[bank_of[stage, 0]], 1)
                return f

            def l0_qk(n):
                def f(g, k):
                    ps = free_bank(g, "l0_" + n, 0, ("l0_xT", 0, 0))
                    pe.matmul(ps[:, :], wT["w" + n][:, :], xT["l0"][:, :], start=True, stop=True)\
                        .then_inc(ring_written[bank_of["l0_" + n, 0]], 1)
                return f

            def l0_v(g, k):
                ps = free_bank(g, "l0_v", 0, ("l0_xT", 0, 0))
                for c in range(C):
                    last = pe.matmul(ps[:, c * D:(c + 1) * D], xT["l0"][:, c * P:(c + 1) * P], wT["wv"][:, :],
                                     start=True, stop=True)
                last.then_inc(ring_written[bank_of["l0_v", 0]], 1)

            def l0_s(g, m):
                c, h = m // HEADS0, m % HEADS0
                if m == 0:
                    pe.wait_ge(signal["q_stacked"], count("q_stacked", g, 128))
                    pe.wait_ge(signal["k_stacked"], count("k_stacked", g, 128))
                wait_if_any(pe, "max0", g, m - 1)
                for q in range(2):
                    last = pe.matmul(ps_s[:, m % 2, :], stack["q"][q][g.p][:, h, c * P:(c + 1) * P],
                                     stack["k"][q][g.p][:, h, :], start=(q == 0), stop=(q == 1))
                last.then_inc(signal["s0_made"], 1)

            def l0_t(g, m):
                pe.wait_ge(signal["exp0"], count("exp0", g, m + 1))
                wait_if_any(pe, "t0_out", g, m - 1)
                for j in range(C):
                    last = pe.transpose(ps_t[:, m % 2, j * P:(j + 1) * P], probs[m // 2 % 2][:, m % 2, j * P:(j + 1) * P],
                                        ident[:, :])
                last.then_inc(signal["t0_made"], 1)

            def l0_pv(g, c):
                pe.wait_ge(signal["t0_out"], count("t0_out", g, 4 * c + 4))
                pe.wait_ge(signal["rden0_made"], count("rden0_made", g, c + 1))
                ps = free_bank(g, "l0_pv", c, *([("l0_v", 0, 0)] if c == 0 else []))
                for j in range(C):
                    for h in range(HEADS0):
                        pe.matmul(ps[DH0 * h:DH0 * (h + 1), 0:P], v0[g.p][:, j, DH0 * h:DH0 * (h + 1)],
                                  probs_t[:, h, j, :], start=(j == 0), stop=(j == C - 1))
                for h in range(HEADS0):
                    last = pe.matmul(ps[DH0 * h:DH0 * (h + 1), P:2 * P],
                                     rden0[:, HEADS0 * c + h:HEADS0 * c + h + 1].broadcast_to([P, DH0]), ident[:, :],
                                     start=True, stop=True)
                last.then_inc(ring_written[bank_of["l0_pv", c]], 1)

            def l0_y(g, k):
                ps = free_bank(g, "l0_y", 0, ("l0_pv", 3, 0))
                for c in range(C):
                    last = pe.matmul(ps[:, c * D:(c + 1) * D], o0_t[:, c * P:(c + 1) * P], wT["wo"][:, :],
                                     start=True, stop=True)
                last.then_inc(ring_written[bank_of["l0_y", 0]], 1)

            def project(stage, src, before, cat, width):
                def f(g, k):
                    ps = free_bank(g, stage, k, (before, 0, 0))
                    for c in range(2):
                        last = pe.matmul(ps[:, c * width:(c + 1) * width], src[:, (2 * k + c) * P:(2 * k + c + 1) * P],
                                         cat[:, 0:width], start=True, stop=True)
                    last.then_inc(ring_written[bank_of[stage, k]], 1)
                return f

            def spread(stage, t, before, parts):
                def f(g, k):
                    ps = free_bank(g, stage, k, *[(before, q, 0) for q in range(parts)])
                    for c in range(C):
                        last = pe.transpose(ps[:, c * P:(c + 1) * P], t[:, c, 1 - k:2 - k].broadcast_to([P, P]), ident[:, :])
                    last.then_inc(ring_written[bank_of[stage, k]], 1)
                return f

            def attend(stage, n, t):
                def f(g, k):
                    pe.wait_ge(signal[n + "_Pm"], count(n + "_Pm", g, 4))
                    ps = free_bank(g, stage, k)
                    for c in range(2):
                        for j in range(C):
                            last = pe.matmul(ps[:, c * (D + 1):(c + 1) * (D + 1)],
                                             gat[n]["P"][:, j, (2 * k + c) * P:(2 * k + c + 1) * P],
                                             t[:, j, 2:3 + D], start=(j == 0), stop=(j == C - 1))
                    last.then_inc(ring_written[bank_of[stage, k]], 1)
                return f

            def l2_dm(g, k):
                ps = free_bank(g, "l2_dm", 0, ("l2_h", 0, 0), ("l2_h", 1, 0))
                for c in range(C):
                    last = pe.transpose(ps[0:HEADS2, c * P:(c + 1) * P], t2[g.p][:, c, D + HEADS2:D + 2 * HEADS2],
                                        ident[:, :])
                last.then_inc(ring_written[bank_of["l2_dm", 0]], 1)

            def l2_db(g, k):
                pe.wait_ge(signal["dmax8_diag"], count("dmax8_diag", g, 1))
                ps = free_bank(g, "l2_db")
                pe.matmul(ps[:, 0:HEADS2], ones[0:HEADS2, :], dmax_diag[:, :], start=True, stop=True)\
                    .then_inc(ring_written[bank_of["l2_db", 0]], 1)

            def l2_s(g, h):
                if h == 0:
                    drained(pe, g, ("l2_h", 0, 0), ("l2_h", 1, 0))
                wait_if_any(pe, "b1_made", g, h)
                for c in range(C):
                    last = pe.transpose(ps_b[:, c * P:(c + 1) * P],
                                        t2[g.p][:, c, D + h:D + h + 1].broadcast_to([P, P]), ident[:, :])
                last.then_inc(signal["s2_made"], 1)

            def l2_v(g, h):
                pe.wait_ge(signal["b1_made"], count("b1_made", g, h + 1))
                if h == 0:
                    pe.wait_ge(signal["gl2"], count("gl2", g, 1))
                wait_if_any(pe, "v2_out", g, h)
                w3 = 3 * W2C
                for c in range(C):
                    for j in range(C):
                        last = pe.matmul(ps_v[:, c * w3:(c + 1) * w3], B1[h % 2][:, j, c * P:(c + 1) * P],
                                         GS[g.p][:, j * HEADS2 + h, :, :].rearrange("p a b -> p (a b)"),
                                         start=(j == 0), stop=(j == C - 1))
                last.then_inc(signal["v2_made"], 1)

            def l2_md(g, k):
                pe.wait_ge(signal["gl2"], count("gl2", g, 1))
                ps = free_bank(g, "l2_md", k)
                wd = HEADS2 * (DH2 + 1)
                for c in range(2):
                    for j in range(C):
                        for q in range(3):
                            last = pe.matmul(ps[:, c * wd:(c + 1) * wd], mask_t[:, j, (2 * k + c) * P:(2 * k + c + 1) * P],
                                             GS[g.p][:, j * HEADS2:(j + 1) * HEADS2, q, DH2 + 1:W2C],
                                             start=(j == 0 and q == 0), stop=(j == C - 1 and q == 2))
                last.then_inc(ring_written[bank_of["l2_md", k]], 1)

            def l2_y(g, k):
                ps = free_bank(g, "l2_y", 0, ("l2_oT", 0, 0))
                for c in range(C):
                    last = pe.matmul(ps[:, c * D:(c + 1) * D], O2_t[:, c * P:(c + 1) * P], wT["w_out"][:, :],
                                     start=True, stop=True)
                last.then_inc(ring_written[bank_of["l2_y", 0]], 1)

            def l3_m1(g, k):
                ps = free_bank(g, "l3_m1", k, ("l3_xT", 0, 0))
                pe.matmul(ps[:, :], w3a[:, k * P:(k + 1) * P], xT["l3"][:, :], start=True, stop=True)\
                    .then_inc(ring_written[bank_of["l3_m1", k]], 1)

            def l3_h(g, c):
                ps = free_bank(g, "l3_h", c, ("l3_m1", 0, 0), ("l3_m1", 1, 0))
                for q in range(2):
                    last = pe.matmul(ps[:, 0:2 + HID], h3_t[:, q, c * P:(c + 1) * P], w3_fc[:, q, :],
                                     start=(q == 0), stop=(q == 1))
                last.then_inc(ring_written[bank_of["l3_h", c]], 1)

            def l3_o(g, c):
                pe.wait_ge(signal["l3_P"], count("l3_P", g, 4))
                ps = free_bank(g, "l3_o", c)
                for j in range(C):
                    last = pe.matmul(ps[:, 0:HID + 1], gat["l3"]["P"][:, j, c * P:(c + 1) * P], t3[:, j, 2:3 + HID],
                                     start=(j == 0), stop=(j == C - 1))
                last.then_inc(ring_written[bank_of["l3_o", c]], 1)

            def l3_zT(g, k):
                pe.wait_ge(signal["z3_made"], count("z3_made", g, 1))
                ps = free_bank(g, "l3_zT", k)
                for c in range(C):
                    last = pe.transpose(ps[:, c * P:(c + 1) * P], v3[:, c, k * P:(k + 1) * P], ident[:, :])
                last.then_inc(ring_written[bank_of["l3_zT", k]], 1)

            def l3_m2(g, k):
                ps = free_bank(g, "l3_m2", 0, ("l3_zT", 0, 0), ("l3_zT", 1, 0))
                for q in range(2):
                    last = pe.matmul(ps[:, :], w3b[:, q, :], h3_t[:, q, :], start=(q == 0), stop=(q == 1))
                last.then_inc(ring_written[bank_of["l3_m2", 0]], 1)

            def l3_r(g, k):
                pe.wait_ge(signal["z4"], count("z4", g, 1))
                ps = free_bank(g, "l3_r", 0, ("l3_m2", 0, 0))
                for c in range(C):
                    last = pe.transpose(ps[:, c * P:(c + 1) * P], out2_t[:, c * P:(c + 1) * P], ident[:, :])
                last.then_inc(ring_written[bank_of["l3_r", 0]], 1)

            run_bodies(pe, SCHEDULE["pe"], {
                "l0_xT": to_T("l0_xT", lambda g: x_in[g.p], lambda g: pe.wait_ge(signal["x_loaded"], count("x_loaded", g, 16))),
                "l0_q": l0_qk("q"), "l0_k": l0_qk("k"), "l0_v": l0_v, "l0_s": l0_s, "l0_t": l0_t, "l0_pv": l0_pv, "l0_y": l0_y,
                "l1_xT": to_T("l1_xT", lambda g: x1[g.p], lambda g: pe.wait_ge(signal["l0_x"], count("l0_x", g, 1))),
                "l1_h": project("l1_h", xT["l1"], "l1_xT", w1_cat, D + 2),
                "l1_sd": spread("l1_sd", t1, "l1_h", 2), "l1_o": attend("l1_o", "l1", t1),
                "l2_xT": to_T("l2_xT", lambda g: x2[g.p], lambda g: pe.wait_ge(signal["l1_x"], count("l1_x", g, 1))),
                "l2_h": project("l2_h", xT["l2"], "l2_xT", w2_cat, D + 2 * HEADS2),
                "l2_dm": l2_dm, "l2_db": l2_db, "l2_s": l2_s, "l2_v": l2_v, "l2_md": l2_md,
                "l2_oT": to_T("l2_oT", lambda g: O2, lambda g: pe.wait_ge(signal["o2_made"], count("o2_made", g, 1))), "l2_y": l2_y,
                "l3_xT": to_T("l3_xT", lambda g: x3[g.p], lambda g: pe.wait_ge(signal["l2_x"], count("l2_x", g, 1))),
                "l3_m1": l3_m1, "l3_h": l3_h, "l3_sd": spread("l3_sd", t3, "l3_h", 4), "l3_o": l3_o,
                "l3_zT": l3_zT, "l3_m2": l3_m2,
                "l3_h2": project("l3_h2", out2_t, "l3_m2", w3_hand, D + 2),
                "l3_r": l3_r, "l3_sd2": spread("l3_sd2", t4, "l3_h2", 2), "l3_o2": attend("l3_o2", "l3b", t4),
            })

        @block.scalar
        def _(act):
            act.preload_act_table_set("natural_log_exp_and_others")
            act.wait_ge(s_pre_pe, 1)
            for n in ("wq", "wk", "wv", "wo"):
                last = act.activation(wT[n][:, :], ring[0][:, RAW[n] * D:(RAW[n] + 1) * D], ACT.Copy)
            last.then_inc(s_pre_act, 1)
            act.activation(wT["w_out"][:, :], ring[1][:, 0:D], ACT.Copy)
            for j in range(C):
                act.wait_ge(s_pre_pe, j + 2)
                act.activation(mask_t[:, j, :], ring[0][:, :], ACT.Copy).then_inc(s_pre_act, 1)
            act.wait_ge(s_pre_dve, 4)
            act.activation(pre[:, 3:4], pre[:, 2:3], ACT.Exp).then_inc(s_pre_act, 1)
            act.wait_ge(s_pre_act, 6)
            act.activation(pre[:, 4:5], pre[:, 3:4], ACT.Ln, bias=1.0)
            act.activation(pre[:, 5:6], ones[:, 0:1], ACT.Ln, bias=pre[:, 6:7]).then_inc(s_setup, 1)
            act.wait_ge(s_setup, 2)

            def xT_out(stage, n, reader, rk):
                def f(g, k):
                    written(act, g, (stage, 0, 0), (reader, rk, 1))
                    act.activation(xT[n][:, :], bank(stage)[:, :], ACT.Copy).then_inc(ring_read[bank_of[stage, 0]], 1)
                return f

            def l0_qk(n, bias):
                def f(g, k):
                    act.wait_ge(ring_written[bank_of["l0_" + n, 0]], uses("l0_" + n, g, 0) + 1)
                    wait_if_any(act, n + "_spilled", g, 16, back=1)
                    act.activation(piece[n][:, 0, :], bank("l0_" + n)[:, :], ACT.Identity, bias=bias[:, 0:1])\
                        .then_inc(signal[n + "_high"], 1)
                return f

            def l0_exp(g, m):
                act.wait_ge(signal["neg_max0"], count("neg_max0", g, m // 2 + 1))
                wait_if_any(act, "rden0_made", g, 4, back=1)
                e = probs[m // 2 % 2][:, m % 2, :]
                act.activation(e, e, ACT.Exp, bias=neg_max[:, m:m + 1], scale=SCALE0, accum_out=den0[:, m:m + 1])\
                    .then_inc(signal["exp0"], 1)

            def l0_t(g, m):
                c, h = m // HEADS0, m % HEADS0
                act.wait_ge(signal["t0_made"], count("t0_made", g, m + 1))
                written(act, g, ("l0_pv", c - 1, 0) if c else ("l0_pv", C - 1, 1))
                act.activation(probs_t[:, h, :, :].rearrange("p j n -> p (j n)"), ps_t[:, m % 2, :], ACT.Copy)\
                    .then_inc(signal["t0_out"], 1)

            def l0_rden(g, c):
                act.wait_ge(ring_written[bank_of["l0_pv", c]], uses("l0_pv", g, c) + 1)
                drained(act, g, ("l0_pv", c - 1, 0) if c else ("l0_pv", C - 1, 1))
                act.activation(rden_t[:, :], bank("l0_pv", c)[:, P:2 * P], ACT.Copy).then_inc(signal["rden0_out"], 1)

            def h_out(stage, t, width, *tickets, old=None):
                def f(g, k):
                    written(act, g, (stage, k, 0), *tickets)
                    if old is not None:
                        old(g)
                    tt = t(g)
                    act.activation(tt[:, 2 * k:2 * k + 2, 0:width],
                                       bank(stage, k)[:, 0:2 * width].rearrange("p (c n) -> p c n", c=2), ACT.Copy)\
                                           .then_inc(ring_read[bank_of[stage, k]], 1)
                return f

            def exp_targets(n):
                def f(g, k):
                    act.wait_ge(signal[n + "_dd"], count(n + "_dd", g, 1))
                    wait_if_any(act, n + "_P", g, 4, back=1)
                    t = gat[n]
                    act.activation(t["b"][:, :], t["dd"][:, :], ACT.Exp).then_inc(signal[n + "_b"], 1)
                    act.activation(t["g"][:, :], t["dd"][:, :], ACT.Exp, scale=0.2).then_inc(signal[n + "_b"], 1)
                return f

            def exp_sources(n, stage):
                def f(g, k):
                    act.wait_ge(ring_read[bank_of[stage, 1]], uses(stage, g, 1) + 1)
                    act.activation(gat[n]["R"][:, :], gat[n]["R"][:, :], ACT.Exp, scale=-0.8).then_inc(signal[n + "_R"], 1)
                return f

            def normalise(n, dst):
                def f(g, k):
                    act.wait_ge(signal[n + "_shift"], count(n + "_shift", g, 1))
                    for c in range(C):
                        last = act.activation(dst[g.p][:, c, :], dst[g.p][:, c, :], ACT.Identity,
                                              bias=shift[n][:, c:c + 1], scale=rstd[n][:, c:c + 1])
                    last.then_inc(signal[n + "_x"], 1)
                return f

            def l2_e(g, k):
                act.wait_ge(signal["small2_made"], count("small2_made", g, 2))
                wait_if_any(act, "g2_made", g, 2, back=1)
                act.activation(bg2[:, 0, :, :], small2[:, 0, :, :], ACT.Exp, bias=ln_prior[:, 0:1])\
                    .then_inc(signal["exp2"], 1)
                act.activation(bg2[:, 1, :, :], small2[:, 0, :, :], ACT.Exp, bias=ln_prior[:, 0:1], scale=0.2)\
                    .then_inc(signal["exp2"], 1)
                wait_if_any(act, "c2", g, 3, back=2)
                act.activation(R2[g.p][:, :, :], small2[:, 1, :, :], ACT.Exp, scale=-0.8).then_inc(signal["exp2"], 1)

            def l2_high(g, k):
                act.wait_ge(signal["g2_made"], count("g2_made", g, 2))
                wait_if_any(act, "v2_made", g, 8, back=2)
                wait_if_any(act, "c2", g, 3, back=2)
                act.activation(GS[g.p][:, :, 0, :], G[:, :, :], ACT.Copy).then_inc(signal["gh2"], 1)

            def l2_v(g, h):
                act.wait_ge(signal["v2_made"], count("v2_made", g, h + 1))
                wait_if_any(act, "u2_made", g, h - 1)
                act.activation(EV[h % 2][:, :, :, :].rearrange("p c q n -> p (c q n)"), ps_v[:, 0:C * 3 * W2C], ACT.Copy)\
                    .then_inc(signal["v2_out"], 1)

            def l2_md(g, k):
                act.wait_ge(ring_written[bank_of["l2_md", k]], uses("l2_md", g, k) + 1)
                wait_if_any(act, "c2", g, 1, back=1)
                wait_if_any(act, "o2_made", g, 1, back=1)
                wd = HEADS2 * (DH2 + 1)
                act.activation(MD[:, 2 * k:2 * k + 2, :], bank("l2_md", k)[:, 0:2 * wd].rearrange("p (c n) -> p c n", c=2),
                                   ACT.Copy).then_inc(ring_read[bank_of["l2_md", k]], 1)

            def l2_oT(g, k):
                written(act, g, ("l2_oT", 0, 0), ("l2_y", 0, 1))
                act.activation(O2_t[:, :], bank("l2_oT")[:, :], ACT.Copy).then_inc(ring_read[bank_of["l2_oT", 0]], 1)

            def l3_m1(g, k):
                written(act, g, ("l3_m1", k, 0), ("l3_m2", 0, 1))
                act.activation(h3_t[:, k, :], bank("l3_m1", k)[:, :], ACT.Relu, bias=b3a[:, k:k + 1])\
                    .then_inc(ring_read[bank_of["l3_m1", k]], 1)

            def l3_h(g, c):
                written(act, g, ("l3_h", c, 0), ("l3_o", C - 1, 1))
                act.activation(t3[:, c, 0:2 + HID], bank("l3_h", c)[:, 0:2 + HID], ACT.Copy)\
                    .then_inc(ring_read[bank_of["l3_h", c]], 1)

            def l3_v(g, c):
                act.wait_ge(signal["l3_rden"], count("l3_rden", g, c + 1))
                written(act, g, ("l3_zT", 1, 1))
                act.activation(v3[:, c, :], bank("l3_o", c)[:, 0:HID], ACT.Copy, scale=gat["l3"]["rden"][:, c:c + 1])\
                    .then_inc(ring_read[bank_of["l3_o", c]], 1)

            def quotient(n, stage, dst, free):
                def f(g, k):
                    act.wait_ge(signal[n + "_rden"], count(n + "_rden", g, k + 1))
                    free(g)
                    for c in range(2):
                        i = 2 * k + c
                        last = act.activation(dst[g.p][:, i, :], bank(stage, k)[:, c * (D + 1):c * (D + 1) + D], ACT.Copy,
                                              scale=gat[n]["rden"][:, i:i + 1])
                    last.then_inc(ring_read[bank_of[stage, k]], 1)
                return f

            def elu(n, v, e, before, parts, old):
                def f(g, k):
                    drained(act, g, *[(before, q, 0) for q in range(parts)])
                    wait_if_any(act, old, g, 1, back=1)
                    act.activation(e[:, :, :], v[:, :, :], ACT.Relu, scale=-1.0).then_inc(signal[f"u{n}_made"], 1)
                    act.wait_ge(signal[f"u{n}_made"], count(f"u{n}_made", g, 1))
                    act.activation(e[:, :, :], e[:, :, :], ACT.Exp, scale=-1.0).then_inc(signal[f"e{n}_first"], 1)
                    act.wait_ge(signal[f"e{n}_first"], count(f"e{n}_first", g, 1))
                    act.activation(e[:, :, :], e[:, :, :], ACT.Exp, bias=neg_one[:, 0:1]).then_inc(signal[f"e{n}_made"], 1)
                return f

            def l3_m2(g, k):
                written(act, g, ("l3_m2", 0, 0), ("l3_r", 0, 1), ("l3_h2", 1, 1))
                act.activation(out2_t[:, :], bank("l3_m2")[:, :], ACT.Relu, bias=b3b[:, 0:1])\
                    .then_inc(ring_read[bank_of["l3_m2", 0]], 1)

            run_bodies(act, SCHEDULE["act"], {
                "l0_xT": xT_out("l0_xT", "l0", "l0_v", 0), "l0_q": l0_qk("q", bias_q), "l0_k": l0_qk("k", bias_k),
                "l0_exp": l0_exp, "l0_t": l0_t, "l0_rden": l0_rden, "l0_norm": normalise("l0", x1),
                "l1_xT": xT_out("l1_xT", "l1", "l1_h", 1),
                "l1_h": h_out("l1_h", lambda g: t1, D + 2, ("l1_o", 1, 1)),
                "l1_e": exp_targets("l1"), "l1_R": exp_sources("l1", "l1_sd"),
                "l1_v": quotient("l1", "l1_o", x2, lambda g: wait_if_any(act, "l2_x", g, 1, back=2)), "l1_norm": normalise("l1", x2),
                "l2_xT": xT_out("l2_xT", "l2", "l2_h", 1),
                "l2_h": h_out("l2_h", lambda g: t2[g.p], D + 2 * HEADS2,
                              old=lambda g: (wait_if_any(act, "s2_made", g, 8, back=2), wait_if_any(act, "g2_made", g, 2, back=2))),
                "l2_e": l2_e, "l2_high": l2_high, "l2_v": l2_v, "l2_md": l2_md, "l2_oT": l2_oT,
                "l2_norm": normalise("l2", x3),
                "l3_xT": xT_out("l3_xT", "l3", "l3_m1", 1), "l3_m1": l3_m1, "l3_h": l3_h,
                "l3_e": exp_targets("l3"), "l3_R": exp_sources("l3", "l3_sd"),
                "l3_v": l3_v, "l3_elu": elu("3", v3, e3, "l3_o", C, "z3_made"), "l3_m2": l3_m2,
                "l3_h2": h_out("l3_h2", lambda g: t4, D + 2, ("l3_o2", 1, 1)),
                "l3_e2": exp_targets("l3b"), "l3_R2": exp_sources("l3b", "l3_sd2"),
                "l3_v2": quotient("l3b", "l3_o2", x4, lambda g: wait_if_any(act, "stored", g, 16, back=1)), "l3_elu2": elu("4", v4, e4, "l3_o2", 2, "z4"), "l3_norm": normalise("l3", x4),
            })

        @block.vector
        def _(dve):
            dve.wait_ge(s_adj, 16)
            adj_p = adj_i.rearrange("p c (q j) -> p c j q", j=C)
            for c in range(C):
                m = mask_add[:, c, :].rearrange("p (j q) -> p j q", j=C)
                dve.tensor_scalar(m, adj_p[:, c, :, :], 0.0, MASKED, ALU.is_equal, ALU.mult)
                last = dve.tensor_scalar(adj_m[:, c, :].rearrange("p (j q) -> p j q", j=C), adj_p[:, c, :, :], 0.0, None,
                                         ALU.is_gt)
            last.then_inc(s_pre_dve, 2)
            dve.wait_ge(s_w, 16 * N_WEIGHT_DMAS)

            tmp = v3[:, :, :].rearrange("p c n -> p (c n)")
            steps = [0]

            def fold_in(dst, wsrc, vec, shape=None):
                n = wsrc.shape[-1] if shape is None else shape[0] * shape[1]
                t = tmp[:, 0:n]
                tv = t if shape is None else t.rearrange("p (h o) -> p h o", h=shape[0])
                steps[0] += 1
                dve.tensor_tensor(t, wsrc, vec, ALU.mult).then_inc(fold_sem, 1)
                dve.wait_ge(fold_sem, steps[0])
                steps[0] += 1
                dve.tensor_reduce(dst, tv, AX_X, ALU.add).then_inc(fold_sem, 1)
                dve.wait_ge(fold_sem, steps[0])

            fold_in(w1_cat[:, 0:1], w1_cat[:, 2:2 + D], foldv[:, 0:D])
            fold_in(w1_cat[:, 1:2], w1_cat[:, 2:2 + D], foldv[:, D:2 * D])
            fold_in(w2_cat[:, D:D + HEADS2], w2_cat[:, 0:D], foldv[:, 256:384], (HEADS2, DH2))
            fold_in(w2_cat[:, D + HEADS2:D + 2 * HEADS2], w2_cat[:, 0:D], foldv[:, 384:512], (HEADS2, DH2))
            for q in range(2):
                fold_in(w3_fc[:, q, 0:1], w3_fc[:, q, 2:2 + HID], foldv[:, 512:768])
                fold_in(w3_fc[:, q, 1:2], w3_fc[:, q, 2:2 + HID], foldv[:, 768:1024])
            fold_in(w3_hand[:, 0:1], w3_hand[:, 2:2 + D], foldv[:, 1024:1152])
            fold_in(w3_hand[:, 1:2], w3_hand[:, 2:2 + D], foldv[:, 1152:1280])
            dve.memset(pre[:, 6:7], PRIOR_EPS)
            dve.tensor_scalar(pre[:, 1:2], pre[:, 0:1], 0.0, None, ALU.max)
            steps[0] += 1
            dve.tensor_scalar(pre[:, 7:8], pre[:, 0:1], -1.0, None, ALU.mult).then_inc(fold_sem, 1)
            dve.wait_ge(fold_sem, steps[0])
            dve.tensor_tensor(pre[:, 2:3], pre[:, 0:1], pre[:, 7:8], ALU.min).then_inc(s_pre_dve, 2)
            dve.wait_ge(s_setup, 1)
            steps[0] += 1
            dve.tensor_tensor(pre[:, 1:2], pre[:, 1:2], pre[:, 4:5], ALU.add).then_inc(fold_sem, 1)
            dve.wait_ge(fold_sem, steps[0])
            dve.wait_ge(s_pre_act, 5)
            dve.tensor_tensor(ln_prior[:, :], pre[:, 1:2], pre[:, 5:6], ALU.mult).then_inc(s_setup, 1)

            def hold_waits(column):
                dve.tensor_copy(waited[:, column:column + 1], neg_half[:, 0:1])

            def l0_qk(n, bias):
                def f(g, k):
                    dve.wait_ge(ring_written[bank_of["l0_" + n, 0]], uses("l0_" + n, g, 0) + 1)
                    dve.wait_ge(signal[n + "_high"], count(n + "_high", g, 1))
                    if n == "q":
                        wait_if_any(dve, "k_split", g, 1, back=1)
                    else:
                        dve.wait_ge(signal["q_split"], count("q_split", g, 1))
                    dve.scalar_tensor_tensor(rest[:, :], bank("l0_" + n)[:, :], bias[:, 0:1], piece[n][:, 0, :],
                                                 ALU.add, ALU.subtract).then_inc(ring_read[bank_of["l0_" + n, 0]], 1)
                return f

            def l0_v(g, k):
                written(dve, g, ("l0_v", 0, 0), ("l0_pv", C - 1, 2))
                dve.tensor_tensor(v0[g.p][:, :, :], bank("l0_v")[:, :].rearrange("p (c n) -> p c n", c=C),
                                      bias_v[:, :].unsqueeze(1).broadcast_to([P, C, D]), ALU.add)\
                                          .then_inc(ring_read[bank_of["l0_v", 0]], 1)

            def l0_max(g, s):
                dve.wait_ge(signal["s0_made"], count("s0_made", g, 2 * s + 2))
                wait_if_any(dve, "t0_made", g, 2 * s - 2)
                wait_if_any(dve, "neg_max0", g, 8, back=1)
                hold_waits(s)
                for h in range(2):
                    dve.tensor_tensor_reduce(probs[s % 2][:, h, :], ps_s[:, h, :], mask_add[:, s // 2, :], 1.0, -3.0e38,
                                                  ALU.add, ALU.max, row_max[:, 2 * s + h:2 * s + h + 1])\
                                                      .then_inc(signal["max0"], 1)

            def l0_neg(g, s):
                dve.wait_ge(signal["max0"], count("max0", g, 2 * s + 2))
                wait_if_any(dve, "exp0", g, 16, back=1)
                dve.tensor_scalar(neg_max[:, 2 * s:2 * s + 2], row_max[:, 2 * s:2 * s + 2], -1.0e20, -SCALE0,
                                       ALU.max, ALU.mult).then_inc(signal["neg_max0"], 1)

            def l0_den(g, c):
                dve.wait_ge(signal["exp0"], count("exp0", g, 4 * c + 4))
                d = den0[:, 4 * c:4 * c + 4]
                dve.tensor_scalar(d, d, 1e-30, None, ALU.max).then_inc(signal["den0_safe"], 1)

            def l0_rcp(g, c):
                dve.wait_ge(signal["den0_safe"], count("den0_safe", g, c + 1))
                written(dve, g, ("l0_pv", c, 1))
                dve.reciprocal(rden0[:, 4 * c:4 * c + 4], den0[:, 4 * c:4 * c + 4]).then_inc(signal["rden0_made"], 1)

            def l0_o(g, c):
                dve.wait_ge(signal["rden0_out"], count("rden0_out", g, c + 1))
                written(dve, g, ("l0_y", 0, 1))
                dve.tensor_tensor(o0_t[:, c * P:(c + 1) * P], bank("l0_pv", c)[:, 0:P], rden_t[:, :], ALU.mult)\
                    .then_inc(ring_read[bank_of["l0_pv", c]], 1)

            def layer_sum(stage, dst, base, more):
                def f(g, k):
                    dve.wait_ge(ring_written[bank_of[stage, 0]], uses(stage, g, 0) + 1)
                    more(g)
                    dve.tensor_tensor(dst[g.p][:, :, :], bank(stage)[:, :].rearrange("p (c n) -> p c n", c=C),
                                          base[g.p][:, :, :], ALU.add).then_inc(ring_read[bank_of[stage, 0]], 1)
                return f

            def bn_stats(n, src, summed):
                def f(g, c):
                    summed(g)
                    wait_if_any(dve, n + "_mv", g, 1, back=1)
                    for c in range(C):
                        last = dve.bn_stats(stats[n][:, c, :], src[g.p][:, c, :])
                    last.then_inc(signal[n + "_stats"], 1)
                return f

            def bn_aggr(n):
                def f(g, k):
                    dve.wait_ge(signal[n + "_stats"], count(n + "_stats", g, 1))
                    wait_if_any(dve, n + "_x", g, 1, back=1)
                    hold_waits(2 * C + int(n[1]))
                    for c in range(C):
                        last = dve.bn_aggr(mv[n][:, c, :], stats[n][:, c, :])
                    last.then_inc(signal[n + "_mv"], 1)
                return f

            def max_target(n, stage):
                def f(g, k):
                    dve.wait_ge(ring_written[bank_of[stage, 0]], uses(stage, g, 0) + 1)
                    drained(dve, g, (stage, 1, 1))
                    wait_if_any(dve, n + "_dd", g, 1, back=1)
                    dve.tensor_reduce(gat[n]["ndmax"][:, :], bank(stage, 0)[:, :], AX_X, ALU.max, negate=True)\
                        .then_inc(ring_read[bank_of[stage, 0]], 1)
                return f

            def target_scores(n, stage, t):
                def f(g, k):
                    dve.wait_ge(ring_read[bank_of[stage, 0]], uses(stage, g, 0) + 1)
                    wait_if_any(dve, n + "_b", g, 2, back=1)
                    dve.tensor_scalar(gat[n]["dd"][:, :], t[:, :, 1], gat[n]["ndmax"][:, 0:1], None, ALU.add)\
                        .then_inc(signal[n + "_dd"], 1)
                return f

            def source_scores(n, stage):
                def f(g, k):
                    dve.wait_ge(ring_read[bank_of[stage, 0]], uses(stage, g, 0) + 1)
                    dve.wait_ge(ring_written[bank_of[stage, 1]], uses(stage, g, 1) + 1)
                    wait_if_any(dve, n + "_P", g, 4, back=1)
                    dve.tensor_scalar(gat[n]["R"][:, :], bank(stage, 1)[:, :], gat[n]["ndmax"][:, 0:1], CAP,
                                          ALU.subtract, ALU.max).then_inc(ring_read[bank_of[stage, 1]], 1)
                return f

            def weights(n, reader, rk):
                def f(g, j):
                    q = gat[n]
                    dve.wait_ge(signal[n + "_R"], count(n + "_R", g, 1))
                    dve.wait_ge(signal[n + "_b"], count(n + "_b", g, 2))
                    written(dve, g, (reader, rk, 1))
                    dve.tensor_scalar(q["P"][:, j, :], q["R"][:, :], q["g"][:, j:j + 1], q["b"][:, j:j + 1],
                                           ALU.mult, ALU.max).then_inc(signal[n + "_P"], 1)
                return f

            def rcp_pair(n, stage):
                def f(g, k):
                    dve.wait_ge(ring_written[bank_of[stage, k]], uses(stage, g, k) + 1)
                    drained(dve, g, (stage, k, 1))
                    dve.reciprocal(gat[n]["rden"][:, 2 * k:2 * k + 2],
                                        bank(stage, k)[:, 0:2 * (D + 1)].rearrange("p (c n) -> p c n", c=2)[:, :, D])\
                                            .then_inc(signal[n + "_rden"], 1)
                return f

            def l2_dm(g, k):
                dve.wait_ge(ring_written[bank_of["l2_dm", 0]], uses("l2_dm", g, 0) + 1)
                wait_if_any(dve, "dmax8_diag", g, 1, back=1)
                dve.tensor_reduce(dmax8[:, :], bank("l2_dm")[0:HEADS2, :], AX_X, ALU.max)\
                    .then_inc(ring_read[bank_of["l2_dm", 0]], 1)

            def l2_diag(g, k):
                dve.wait_ge(ring_read[bank_of["l2_dm", 0]], uses("l2_dm", g, 0) + 1)
                written(dve, g, ("l2_db", 0, 1))
                dve.tensor_scalar(dmax_diag[:, :], ident[0:HEADS2, 0:HEADS2], dmax8[:, 0:1], None, ALU.mult)\
                    .then_inc(signal["dmax8_diag"], 1)

            def l2_db(g, k):
                dve.wait_ge(ring_written[bank_of["l2_db", 0]], uses("l2_db", g, 0) + 1)
                wait_if_any(dve, "small2_made", g, 2, back=1)
                dve.tensor_copy(dmax_all[:, :], bank("l2_db")[:, 0:HEADS2]).then_inc(ring_read[bank_of["l2_db", 0]], 1)

            def l2_small(g, k):
                dve.wait_ge(ring_read[bank_of["l2_db", 0]], uses("l2_db", g, 0) + 1)
                d = t2[g.p][:, :, D + HEADS2:D + 2 * HEADS2]
                s = t2[g.p][:, :, D:D + HEADS2]
                m = dmax_all[:, :].unsqueeze(1).broadcast_to([P, C, HEADS2])
                wait_if_any(dve, "exp2", g, 3, back=1)
                wait_if_any(dve, "b1_made", g, 8, back=2)
                dve.tensor_tensor(small2[:, 0, :, :], d, m, ALU.subtract)
                dve.tensor_scalar(neg_d[g.p][:, :, :], d, -1.0, None, ALU.mult)
                dve.tensor_tensor(small2[:, 1, :, :], s, m, ALU.add).then_inc(signal["small2_made"], 1)

            def l2_cap(g, k):
                dve.wait_ge(signal["small2_made"], count("small2_made", g, 1))
                dve.tensor_scalar(small2[:, 1, :, :], small2[:, 1, :, :], CAP, None, ALU.max)\
                    .then_inc(signal["small2_made"], 1)

            def l2_signs(g, h):
                dve.wait_ge(signal["s2_made"], count("s2_made", g, h + 1))
                dve.wait_ge(signal["small2_made"], count("small2_made", g, 1))
                wait_if_any(dve, "v2_made", g, h - 1)
                for j in range(C):
                    last = dve.scalar_tensor_tensor(B1[h % 2][:, j, :], ps_b[:, :], neg_d[g.p][:, j, h:h + 1],
                                                    mask_t[:, j, :], ALU.is_ge, ALU.mult)
                last.then_inc(signal["b1_made"], 1)

            def l2_rcp(g, k):
                dve.wait_ge(signal["c2"], count("c2", g, 3))
                wait_if_any(dve, "o2_made", g, 1, back=1)
                hv = MD[:, :, :].rearrange("p c (h n) -> p (c h) n", h=HEADS2)
                dve.reciprocal(rden2[:, :, :].rearrange("p c h -> p (c h)"), hv[:, :, DH2])\
                    .then_inc(signal["rden2_made"], 1)

            def l3_rcp(g, c):
                dve.wait_ge(ring_written[bank_of["l3_o", c]], uses("l3_o", g, c) + 1)
                drained(dve, g, ("l3_o", c, 1))
                dve.reciprocal(gat["l3"]["rden"][:, c:c + 1], bank("l3_o", c)[:, HID:HID + 1])\
                    .then_inc(signal["l3_rden"], 1)

            def l3_z(g, k):
                dve.wait_ge(signal["e3_made"], count("e3_made", g, 1))
                dve.scalar_tensor_tensor(v3[:, :, :], e3[:, :, :], -1.0, v3[:, :, :], ALU.add, ALU.max)\
                    .then_inc(signal["z3_made"], 1)

            def l3_zT(g, k):
                dve.wait_ge(ring_written[bank_of["l3_zT", k]], uses("l3_zT", g, k) + 1)
                dve.tensor_tensor(h3_t[:, k, :], bank("l3_zT", k)[:, :], h3_t[:, k, :], ALU.add)\
                    .then_inc(ring_read[bank_of["l3_zT", k]], 1)

            def l3_z2(g, k):
                dve.wait_ge(signal["e4_made"], count("e4_made", g, 1))
                dve.scalar_tensor_tensor(v4[:, :, :], e4[:, :, :], -1.0, v4[:, :, :], ALU.add, ALU.max)\
                    .then_inc(signal["z4"], 1)

            def l3_sum(g, k):
                dve.wait_ge(signal["z4"], count("z4", g, 1))
                dve.wait_ge(ring_written[bank_of["l3_r", 0]], uses("l3_r", g, 0) + 1)
                dve.tensor_tensor(v4[:, :, :], v4[:, :, :], bank("l3_r")[:, :].rearrange("p (c n) -> p c n", c=C), ALU.add)\
                    .then_inc(ring_read[bank_of["l3_r", 0]], 1)

            def l3_y(g, k):
                dve.wait_ge(ring_read[bank_of["l3_r", 0]], uses("l3_r", g, 0) + 1)
                dve.scalar_tensor_tensor(x4[g.p][:, :, :], v4[:, :, :], 0.0, x3[g.p][:, :, :], ALU.max, ALU.add)\
                    .then_inc(signal["x4_made"], 1)

            run_bodies(dve, SCHEDULE["dve"], {
                "l0_q": l0_qk("q", bias_q), "l0_k": l0_qk("k", bias_k), "l0_v": l0_v, "l0_max": l0_max, "l0_neg": l0_neg,
                "l0_den": l0_den, "l0_rcp": l0_rcp, "l0_o": l0_o,
                "l0_y": layer_sum("l0_y", x1, x_in, lambda g: (dve.wait_ge(signal["x_biased"], count("x_biased", g, 1)), wait_if_any(dve, "l1_x", g, 1, back=2))),
                "l0_stats": bn_stats("l0", x1, lambda g: dve.wait_ge(ring_read[bank_of["l0_y", 0]], uses("l0_y", g, 0) + 1)), "l0_aggr": bn_aggr("l0"),
                "l1_dmax": max_target("l1", "l1_sd"), "l1_dd": target_scores("l1", "l1_sd", t1),
                "l1_s": source_scores("l1", "l1_sd"), "l1_p": weights("l1", "l1_o", 1),
                "l1_rcp": rcp_pair("l1", "l1_o"),
                "l1_stats": bn_stats("l1", x2, lambda g: dve.wait_ge(signal["x2_made"], count("x2_made", g, 1))), "l1_aggr": bn_aggr("l1"),
                "l2_dm": l2_dm, "l2_diag": l2_diag, "l2_db": l2_db, "l2_small": l2_small, "l2_cap": l2_cap,
                "l2_signs": l2_signs, "l2_rcp": l2_rcp,
                "l2_y": layer_sum("l2_y", x3, x2, lambda g: wait_if_any(dve, "l3_x", g, 1, back=2)),
                "l2_stats": bn_stats("l2", x3, lambda g: dve.wait_ge(ring_read[bank_of["l2_y", 0]], uses("l2_y", g, 0) + 1)), "l2_aggr": bn_aggr("l2"),
                "l3_dmax": max_target("l3", "l3_sd"), "l3_dd": target_scores("l3", "l3_sd", t3),
                "l3_s": source_scores("l3", "l3_sd"), "l3_p": weights("l3", "l3_o", 3), "l3_rcp": l3_rcp, "l3_z": l3_z,
                "l3_zT": l3_zT,
                "l3_dmax2": max_target("l3b", "l3_sd2"), "l3_dd2": target_scores("l3b", "l3_sd2", t4),
                "l3_s2": source_scores("l3b", "l3_sd2"), "l3_p2": weights("l3b", "l3_o2", 1),
                "l3_rcp2": rcp_pair("l3b", "l3_o2"), "l3_z2": l3_z2, "l3_sum": l3_sum, "l3_y": l3_y,
                "l3_stats": bn_stats("l3", x4, lambda g: dve.wait_ge(signal["x4_made"], count("x4_made", g, 1))), "l3_aggr": bn_aggr("l3"),
            })

        @block.gpsimd
        def _(pool):
            pool.memset(ident[:, :], 0.0).then_inc(s_const, 1)
            pool.memset(ones[:, :], 1.0)
            pool.memset(neg_half[:, :], -0.5)
            pool.memset(neg_one[:, :], -1.0)
            pool.memset(ln_eps[:, :], LN_EPS)
            pool.memset(t1[:, :, D + 2:D + 3], 1.0)
            pool.memset(t4[:, :, D + 2:D + 3], 1.0)
            pool.memset(t3[:, :, HID + 2:HID + 3], 1.0).then_inc(s_const, 1)
            pool.wait_ge(s_const, 2)
            pool.affine_select(out=ident[:, :], in_=ident[:, :], compare_op=ALU.not_equal, fill=1.0, base=0,
                               pattern=[[-1, P]], channel_multiplier=1).then_inc(s_const, 1)
            pool.wait_ge(s_const, 3)
            pool.wait_ge(s_setup, 2)

            def l0_bias(g, k):
                pool.wait_ge(signal["x_loaded"], count("x_loaded", g, 16))
                pool.wait_ge(ring_written[bank_of["l0_xT", 0]], uses("l0_xT", g, 0) + 1)
                pool.tensor_tensor(x_in[g.p][:, :, :], x_in[g.p][:, :, :],
                                        bias_o[:, :].unsqueeze(1).broadcast_to([P, C, D]), ALU.add)\
                                            .then_inc(signal["x_biased"], 1)

            def l0_qk(n):
                def f(g, k):
                    if k == 0:
                        pool.wait_ge(ring_read[bank_of["l0_" + n, 0]], uses("l0_" + n, g, 0) + 1)
                        wait_if_any(pool, n + "_spilled", g, 16, back=1)
                        pool.tensor_tensor(piece[n][:, 1, :], rest[:, :], ones[:, 0:1].broadcast_to([P, N_NODES]), ALU.mult)\
                            .then_inc(signal[n + "_mid"], 1)
                    else:
                        pool.wait_ge(signal[n + "_mid"], count(n + "_mid", g, 1))
                        pool.tensor_tensor(piece[n][:, 2, :], rest[:, :], piece[n][:, 1, :], ALU.subtract)\
                            .then_inc(signal[n + "_split"], 1)
                return f

            def variance(n):
                def f(g, k):
                    pool.wait_ge(signal[n + "_mv"], count(n + "_mv", g, 1))
                    wait_if_any(pool, n + "_x", g, 1, back=1)
                    pool.tensor_tensor(rstd[n][:, :], mv[n][:, :, 1], ln_eps[:, :], ALU.add).then_inc(signal[n + "_var"], 1)
                    pool.tensor_tensor(shift[n][:, :], mv[n][:, :, 0], neg_one[:, :], ALU.mult)\
                        .then_inc(signal[n + "_var"], 1)
                return f

            def power(n):
                def f(g, k):
                    pool.wait_ge(signal[n + "_var"], count(n + "_var", g, 2))
                    pool.tensor_tensor(rstd[n][:, :], rstd[n][:, :], neg_half[:, :], ALU.pow)\
                        .then_inc(signal[n + "_rstd"], 1)
                return f

            def shifts(n):
                def f(g, k):
                    pool.wait_ge(signal[n + "_rstd"], count(n + "_rstd", g, 1))
                    pool.tensor_tensor(shift[n][:, :], shift[n][:, :], rstd[n][:, :], ALU.mult)\
                        .then_inc(signal[n + "_shift"], 1)
                return f

            def l1_y(g, k):
                drained(pool, g, ("l1_o", 0, 0), ("l1_o", 1, 0))
                pool.wait_ge(signal["l0_x"], count("l0_x", g, 1))
                pool.tensor_tensor(x2[g.p][:, :, :], x2[g.p][:, :, :], x1[g.p][:, :, :], ALU.add)\
                    .then_inc(signal["x2_made"], 1)

            def mask_weights(n):
                def f(g, j):
                    pool.wait_ge(signal[n + "_P"], count(n + "_P", g, j + 1))
                    t = gat[n]["P"][:, j, :]
                    pool.tensor_tensor(t, t, mask_t[:, j, :], ALU.mult).then_inc(signal[n + "_Pm"], 1)
                return f

            def l2_g(g, q):
                pool.wait_ge(signal["exp2"], count("exp2", g, 3))
                wait_if_any(pool, "gl2", g, 1, back=1)
                h = t2[g.p][:, :, 0:D].rearrange("p c (h o) -> p c h o", h=HEADS2)
                G4 = G[:, :, :].rearrange("p (c h) n -> p c h n", c=C)
                e = bg2[:, q, :, :]
                pool.tensor_tensor(G4[:, :, :, q * (DH2 + 1):q * (DH2 + 1) + DH2], h,
                                       e.unsqueeze(3).broadcast_to([P, C, HEADS2, DH2]), ALU.mult)
                pool.tensor_tensor(G4[:, :, :, q * (DH2 + 1) + DH2], e, ones[:, 0:C * HEADS2].rearrange("p (c h) -> p c h", c=C),
                                        ALU.mult).then_inc(signal["g2_made"], 1)

            def l2_split(g, k):
                if k == 0:
                    pool.wait_ge(signal["gh2"], count("gh2", g, 1))
                    pool.tensor_tensor(G[:, :, :], G[:, :, :], GS[g.p][:, :, 0, :], ALU.subtract).then_inc(signal["gr2"], 1)
                elif k == 1:
                    pool.wait_ge(signal["gr2"], count("gr2", g, 1))
                    pool.tensor_tensor(GS[g.p][:, :, 1, :], G[:, :, :],
                                            ones[:, 0:1].unsqueeze(2).broadcast_to([P, C * HEADS2, W2C]), ALU.mult)\
                                                .then_inc(signal["gm2"], 1)
                else:
                    pool.wait_ge(signal["gm2"], count("gm2", g, 1))
                    pool.tensor_tensor(GS[g.p][:, :, 2, :], G[:, :, :], GS[g.p][:, :, 1, :], ALU.subtract)\
                        .then_inc(signal["gl2"], 1)

            def l2_u(g, h):
                pool.wait_ge(signal["v2_out"], count("v2_out", g, h + 1))
                wait_if_any(pool, "c2", g, 3, back=1)
                e = EV[h % 2]
                pool.tensor_tensor(U[:, h, :, :], e[:, :, 0, :], e[:, :, 1, :], ALU.add).then_inc(signal["u2_first"], 1)

            def l2_w(g, h):
                pool.wait_ge(signal["u2_first"], count("u2_first", g, h + 1))
                pool.tensor_tensor(U[:, h, :, :], U[:, h, :, :], EV[h % 2][:, :, 2, :], ALU.add)\
                    .then_inc(signal["u2_made"], 1)

            def l2_c(g, k):
                mm = MD[:, :, :].rearrange("p c (h n) -> p (c h) n", h=HEADS2)
                if k == 1:
                    pool.wait_ge(signal["c2"], count("c2", g, 1))
                    pool.tensor_tensor(mm, mm, R2[g.p][:, :, :].rearrange("p c h -> p (c h)").unsqueeze(2)
                                            .broadcast_to([P, C * HEADS2, DH2 + 1]), ALU.mult).then_inc(signal["c2"], 1)
                    return
                if k == 0:
                    pool.wait_ge(signal["u2_made"], count("u2_made", g, 8))
                    drained(pool, g, ("l2_md", 0, 0), ("l2_md", 1, 0))
                else:
                    pool.wait_ge(signal["c2"], count("c2", g, 2))
                for c in range(C):
                    mc = MD[:, c, :].rearrange("p (h n) -> p h n", h=HEADS2)
                    if k == 0:
                        last = pool.tensor_tensor(mc, mc, U[:, :, c, DH2 + 1:W2C], ALU.subtract)
                    else:
                        last = pool.tensor_tensor(mc, mc, U[:, :, c, 0:DH2 + 1], ALU.add)
                last.then_inc(signal["c2"], 1)

            def l2_o(g, k):
                hv = MD[:, :, :].rearrange("p c (h n) -> p (c h) n", h=HEADS2)
                pool.wait_ge(signal["rden2_made"], count("rden2_made", g, 1))
                written(pool, g, ("l2_oT", 0, 1))
                pool.tensor_tensor(O2[:, :, :].rearrange("p c (h o) -> p (c h) o", h=HEADS2), hv[:, :, 0:DH2],
                                       rden2[:, :, :].rearrange("p c h -> p (c h)").unsqueeze(2)
                                       .broadcast_to([P, C * HEADS2, DH2]), ALU.mult).then_inc(signal["o2_made"], 1)

            layer_norms = {}
            for n in ("l0", "l1", "l2", "l3"):
                layer_norms.update({n + "_var": variance(n), n + "_pow": power(n), n + "_shift": shifts(n)})
            run_bodies(pool, SCHEDULE["pool"], {
                **layer_norms, "l0_bias": l0_bias, "l0_q": l0_qk("q"), "l0_k": l0_qk("k"),
                "l1_y": l1_y, "l1_mask": mask_weights("l1"), "l3_mask2": mask_weights("l3b"), "l2_g": l2_g, "l2_split": l2_split, "l2_o": l2_o,
                "l2_u": l2_u, "l2_w": l2_w, "l2_c": l2_c,
            })


_WEIGHTS = ['L0_gnn_wq', 'L0_gnn_bq', 'L0_gnn_wk', 'L0_gnn_bk', 'L0_gnn_wv', 'L0_gnn_bv', 'L0_gnn_wo', 'L0_gnn_bo',
            'L1_gnn_W', 'L1_gnn_a', 'L2_gnn_W', 'L2_gnn_a_src', 'L2_gnn_a_dst', 'L2_gnn_beta_tilde', 'L2_gnn_W_out',
            'L3_gnn_mlp1_w', 'L3_gnn_mlp1_b', 'L3_gnn_mlp2_w', 'L3_gnn_mlp2_b', 'L3_gnn_W_fc', 'L3_gnn_a_fc',
            'L3_gnn_W_hand', 'L3_gnn_a_hand']


def kernel(**inputs):
    import numpy as _np
    import concourse.bacc as _bacc
    from concourse import mybir as _mybir
    from concourse.bass_utils import run_bass_kernel_spmd as _run

    nc = _bacc.Bacc("TRN2", target_bir_lowering=False, num_devices=1)
    arrays, aps = {}, {}
    for name in ['x', 'adj'] + _WEIGHTS:
        a = _np.atleast_1d(_np.asarray(inputs[name]))
        a = _np.ascontiguousarray(a)
        arrays[f"in_{name}"] = a
        aps[name] = nc.dram_tensor(f"in_{name}", a.shape, _mybir.dt.from_np(a.dtype), kind="ExternalInput").ap()
    out = nc.dram_tensor("out", (N_GRAPHS, N_NODES, D), F32, kind="ExternalOutput").ap()
    build_program(nc, aps['x'], aps['adj'], {n: aps[n] for n in _WEIGHTS}, out)
    r = _run(nc, [arrays], core_ids=[0])
    return _np.asarray(r.results[0]["out"])
```
